# Optimizing a Trainium2 kernel written in Bass

```python
import numpy as np
import jax
import jax.numpy as jnp

def _softmax(x, axis=-1):
    return jax.nn.softmax(x, axis=axis)

def _gelu(x):
    return jax.nn.gelu(x, approximate=True)

def _silu(x):
    return jax.nn.silu(x)

def _sigmoid(x):
    return jax.nn.sigmoid(x)

def _layernorm(x, axis=-1, eps=1e-05):
    m = jnp.mean(x, axis=axis, keepdims=True)
    v = jnp.var(x, axis=axis, keepdims=True)
    return (x - m) / jnp.sqrt(v + eps)

def _scatter_add(tgt, idx, src, axis=0):
    return tgt.at[idx].add(src)

def _segment_sum(src, seg, n):
    return jax.ops.segment_sum(src, seg, n)
kernel_name = 'mk_prb_d1_jaxref_r8_0b5f7f'

def setup_inputs(seed: int=0):
    np.random.seed(seed)
    _w = jnp.asarray

    def _L0_attn_setup():
        import jax, jax.numpy as jnp
        import numpy as np
        EMBED = 128
        HEADS = 16
        HD = EMBED // HEADS
        M = 32
        R = 2
        EPS = 1e-06
        C_CONST = 2.0 + EPS
        CHUNK = 64

        def _features(x, omega, quad_nodes, quad_weights):
            B, H, T, D = x.shape
            xn = x / jnp.maximum(jnp.linalg.norm(x, axis=-1, keepdims=True), 1e-12)
            proj = jnp.einsum('bhtd,rhdm->rbhtm', xn, omega)
            s = quad_nodes[:, None, None, None, None]
            sqrt_2s = jnp.sqrt(2.0 * jnp.maximum(s, 0.0))
            arg = jnp.clip(proj * sqrt_2s - s, -20.0, 20.0)
            feat = jnp.exp(arg) / np.sqrt(M).astype(np.float32)
            feat = feat * jnp.sqrt(jnp.maximum(quad_weights, 0.0))[:, None, None, None, None]
            return jnp.transpose(feat, (1, 2, 3, 0, 4)).reshape(B, H, T, R * M)
        key = jax.random.key(seed)
        ks = jax.random.split(key, 4)
        B, T = (2, 256)
        x = jax.random.normal(ks[0], (B, T, EMBED), jnp.float32)
        Wqkv = jax.random.normal(ks[1], (EMBED, 3 * EMBED), jnp.float32) * 0.02
        bqkv = jnp.zeros((3 * EMBED,), jnp.float32)
        Wout = jax.random.normal(ks[2], (EMBED, EMBED), jnp.float32) * 0.02
        bout = jnp.zeros((EMBED,), jnp.float32)
        omega = jax.random.normal(ks[3], (R, HEADS, HD, M), jnp.float32)
        nodes, weights = np.polynomial.laguerre.laggauss(R)
        quad_nodes = jnp.asarray(nodes / C_CONST, jnp.float32)
        quad_weights = jnp.asarray(weights * (C_CONST / 4.0), jnp.float32)
        return {'x': x, 'Wqkv': Wqkv, 'bqkv': bqkv, 'Wout': Wout, 'bout': bout, 'omega': omega, 'quad_nodes': quad_nodes, 'quad_weights': quad_weights}
    _L0_attn_in = _L0_attn_setup()

    def _L0_ffn_setup():
        import jax, jax.numpy as jnp
        import numpy as np
        EPS = 1e-12

        def rms_norm(t, gamma):
            n = jnp.maximum(jnp.linalg.norm(t, axis=-1, keepdims=True), EPS)
            scale = jnp.sqrt(jnp.asarray(t.shape[-1], t.dtype))
            return t / n * scale * gamma
        key = jax.random.key(seed)
        ks = jax.random.split(key, 4)
        b, s, d = (4, 512, 128)
        e, t = (8, 64)
        hidden = 4 * d
        return {'x': jax.random.normal(ks[0], (b, s, d), dtype=jnp.float32), 'gamma_x': jnp.ones((d,), dtype=jnp.float32), 'gamma_slot': jnp.ones((d,), dtype=jnp.float32), 'slot_embeds': jax.random.normal(ks[1], (e, t, d), dtype=jnp.float32), 'w1': jax.random.normal(ks[2], (d, hidden), dtype=jnp.float32) * (1.0 / np.sqrt(d)), 'w2': jax.random.normal(ks[3], (hidden, d), dtype=jnp.float32) * (1.0 / np.sqrt(hidden))}
    _L0_ffn_in = _L0_ffn_setup()
    _d = {'L0_attn_x': _L0_attn_in['x'], 'L0_attn_Wqkv': _L0_attn_in['Wqkv'], 'L0_attn_bqkv': _L0_attn_in['bqkv'], 'L0_attn_Wout': _L0_attn_in['Wout'], 'L0_attn_bout': _L0_attn_in['bout'], 'L0_attn_omega': _L0_attn_in['omega'], 'L0_attn_quad_nodes': _L0_attn_in['quad_nodes'], 'L0_attn_quad_weights': _L0_attn_in['quad_weights'], 'L0_ffn_gamma_x': _L0_ffn_in['gamma_x'], 'L0_ffn_gamma_slot': _L0_ffn_in['gamma_slot'], 'L0_ffn_slot_embeds': _L0_ffn_in['slot_embeds'], 'L0_ffn_w1': _L0_ffn_in['w1'], 'L0_ffn_w2': _L0_ffn_in['w2']}
    _x0 = _d['L0_attn_x']
    _d['L0_attn_x'] = jax.random.normal(jax.random.fold_in(jax.random.key(seed), 1), (16, 256, 128), dtype=_x0.dtype)
    del _x0
    return _d

def reference(L0_attn_x, L0_attn_Wqkv, L0_attn_bqkv, L0_attn_Wout, L0_attn_bout, L0_attn_omega, L0_attn_quad_nodes, L0_attn_quad_weights, L0_ffn_gamma_x, L0_ffn_gamma_slot, L0_ffn_slot_embeds, L0_ffn_w1, L0_ffn_w2):

    def _L0_attn_ref(x, Wqkv, bqkv, Wout, bout, omega, quad_nodes, quad_weights):
        import jax, jax.numpy as jnp
        import numpy as np
        EMBED = 128
        HEADS = 16
        HD = EMBED // HEADS
        M = 32
        R = 2
        EPS = 1e-06
        C_CONST = 2.0 + EPS
        CHUNK = 64

        def _features(x, omega, quad_nodes, quad_weights):
            B, H, T, D = x.shape
            xn = x / jnp.maximum(jnp.linalg.norm(x, axis=-1, keepdims=True), 1e-12)
            proj = jnp.einsum('bhtd,rhdm->rbhtm', xn, omega)
            s = quad_nodes[:, None, None, None, None]
            sqrt_2s = jnp.sqrt(2.0 * jnp.maximum(s, 0.0))
            arg = jnp.clip(proj * sqrt_2s - s, -20.0, 20.0)
            feat = jnp.exp(arg) / np.sqrt(M).astype(np.float32)
            feat = feat * jnp.sqrt(jnp.maximum(quad_weights, 0.0))[:, None, None, None, None]
            return jnp.transpose(feat, (1, 2, 3, 0, 4)).reshape(B, H, T, R * M)
        B, T, C = x.shape
        qkv = x @ Wqkv + bqkv
        q, k, v = jnp.split(qkv, 3, axis=-1)
        resh = lambda t: t.reshape(B, T, HEADS, HD).transpose(0, 2, 1, 3)
        q, k, v = (resh(q), resh(k), resh(v))
        qf = _features(q, omega, quad_nodes, quad_weights)
        kf = _features(k, omega, quad_nodes, quad_weights)
        Fd = R * M
        nc = T // CHUNK
        to_chunks = lambda t, last: t.reshape(B, HEADS, nc, CHUNK, last).transpose(2, 0, 1, 3, 4)
        qc = to_chunks(qf, Fd)
        kc = to_chunks(kf, Fd)
        vc = to_chunks(v, HD)

        def step(carry, inp):
            kv_state, k_state = carry
            q_ch, k_ch, v_ch = inp
            kv_prod = jnp.einsum('bhtf,bhtd->bhtfd', k_ch, v_ch)
            kv_cur = jnp.cumsum(kv_prod, axis=2) + kv_state[:, :, None]
            k_cur = jnp.cumsum(k_ch, axis=2) + k_state[:, :, None]
            ctx = jnp.einsum('bhtf,bhtfd->bhtd', q_ch, kv_cur)
            den = jnp.maximum(jnp.einsum('bhtf,bhtf->bht', q_ch, k_cur), 1e-06)
            out_ch = ctx / den[..., None]
            return ((kv_cur[:, :, -1], k_cur[:, :, -1]), out_ch)
        init = (jnp.zeros((B, HEADS, Fd, HD), jnp.float32), jnp.zeros((B, HEADS, Fd), jnp.float32))
        _, outs = jax.lax.scan(step, init, (qc, kc, vc))
        out = outs.transpose(1, 2, 0, 3, 4).reshape(B, HEADS, T, HD)
        out = out.transpose(0, 2, 1, 3).reshape(B, T, C)
        return out @ Wout + bout

    def _L0_ffn_ref(x, gamma_x, gamma_slot, slot_embeds, w1, w2):
        import jax, jax.numpy as jnp
        import numpy as np
        EPS = 1e-12

        def rms_norm(t, gamma):
            n = jnp.maximum(jnp.linalg.norm(t, axis=-1, keepdims=True), EPS)
            scale = jnp.sqrt(jnp.asarray(t.shape[-1], t.dtype))
            return t / n * scale * gamma
        b, s, d = x.shape
        e, t, _ = slot_embeds.shape
        xn = rms_norm(x, gamma_x)
        se = rms_norm(slot_embeds, gamma_slot)
        logits = jnp.einsum('bsd,etd->bset', xn, se)
        dispatch = jax.nn.softmax(logits, axis=1)
        slots = jnp.einsum('bsd,bset->betd', xn, dispatch)
        h = jax.nn.gelu(slots @ w1, approximate=False)
        processed = h @ w2
        combine = jax.nn.softmax(logits.reshape(b, s, e * t), axis=-1)
        out = jnp.einsum('bnd,bsn->bsd', processed.reshape(b, e * t, d), combine)
        return out
    x = L0_attn_x
    xn = _layernorm(x, axis=-1)
    x = x + _L0_attn_ref(xn, L0_attn_Wqkv, L0_attn_bqkv, L0_attn_Wout, L0_attn_bout, L0_attn_omega, L0_attn_quad_nodes, L0_attn_quad_weights) + _L0_ffn_ref(xn, L0_ffn_gamma_x, L0_ffn_gamma_slot, L0_ffn_slot_embeds, L0_ffn_w1, L0_ffn_w2)
    return x

_drawn_inputs = setup_inputs


def setup_inputs(seed=0):
    import zlib

    import numpy as np

    out = dict(_drawn_inputs(seed))
    spreads = {'L0_attn_bqkv': (0.0, 0.371),
     'L0_attn_bout': (0.0, 0.1),
     'L0_ffn_gamma_x': (1.0, 0.2),
     'L0_ffn_gamma_slot': (1.0, 0.2)}
    factors = {'L0_attn_Wqkv': 7.457,
     'L0_attn_omega': 8.0,
     'L0_attn_quad_nodes': 8.0,
     'L0_attn_quad_weights': 8.0}
    for name, (base, spread) in spreads.items():
        noise = np.random.default_rng([zlib.crc32(name.encode()), seed]).standard_normal(out[name].shape)
        drawn = base * np.exp(spread * noise) if base else spread * noise
        out[name] = jnp.asarray(drawn.astype(out[name].dtype))
    for name, factor in factors.items():
        out[name] = (out[name] * factor).astype(out[name].dtype)
    return out
```

```python
from contextlib import ExitStack

import concourse.bass as bass
from concourse import mybir

F32 = mybir.dt.float32
F32R = mybir.dt.float32r
F16 = mybir.dt.float16
BF16 = mybir.dt.bfloat16
ALU = mybir.AluOpType
ACT = mybir.ActivationFunctionType
AX_X = mybir.AxisListType.X

B, T, C = 16, 256, 128
HEADS, HD = 16, 8
R, M = 2, 32
PAIRS = HEADS // 2
GROUPS = 2
GP = PAIRS // GROUPS
TILES = T // 128
SLOTS = 512
NCH = SLOTS // 128
HID = 512
MCH = HID // 128
LN_EPS = 1e-5
NORM_FLOOR = 1e-24
DEN_FLOOR = 1e-6
CLIP = 20.0


def count(b, per, extra):
    i, u = b
    if isinstance(i, int):
        return (2 * i + u) * per + extra
    return i * (2 * per) + (u * per + extra)


def landed(b, extra):
    i, u = b
    return i * 16 + 16 * extra


def after(eng, sem, value):
    if isinstance(value, int) and value <= 0:
        return
    eng.wait_ge(sem, value)


def hold(eng, sem, value):
    if isinstance(value, int) and value <= 0:
        return
    eng.wait_ge(sem, value)
    eng.nop(nofuse=True)


def step(b, k):
    i, u = b
    u += k
    return (i + u // 2, u % 2)


def run_rows(eng, row):
    for u in range(2):
        row((0, u), u == 0, True, True)
    with eng.Fori(1, B // 2 - 1) as i:
        for u in range(2):
            row((i, u), False, True, True)
    for u in range(2):
        row((B // 2 - 1, u), False, u == 0, False)


def build(nc, x, Wqkv, bqkv, Wout, bout, omega, nodes, weights, gamma_x, gamma_slot, slot_embeds,
          w1, w2, out):
    with ExitStack() as ctx:
        def sb(name, shape, dt=F32):
            return ctx.enter_context(nc.sbuf_tensor(name, shape, dt))

        def pb(name, shape):
            return ctx.enter_context(nc.psum_tensor(name, shape, F32))

        def sem(name):
            return ctx.enter_context(nc.semaphore(name))

        ident = sb("ident", [128, 128])
        ident16 = sb("ident16", [128, 128], F16)
        neg_ident = sb("neg_ident", [128, 128], BF16)
        causal = sb("causal", [128, 128])
        head_mask = sb("head_mask", [128, 2])
        wqkv_f = sb("wqkv_f", [128, 384])
        wqkv_hi = sb("wqkv_hi", [128, 384], F32R)
        wqkv_lo = sb("wqkv_lo", [128, 384], F32R)
        w1_f = sb("w1_f", [128, HID])
        w1_hi = sb("w1_hi", [128, HID], F32R)
        w1_lo = sb("w1_lo", [128, HID], F32R)
        w2_sb = sb("w2_sb", [128, MCH, 128])
        wout_sb = sb("wout_sb", [128, 128])
        bqkv_bc = sb("bqkv_bc", [128, 384])
        bout_bc = sb("bout_bc", [128, 128])
        gx_bc = sb("gx_bc", [128, 128])
        gs_bc = sb("gs_bc", [128, 128])
        gx_rt = sb("gx_rt", [128, 128])
        gs_rt = sb("gs_rt", [128, 128])
        se_rows = sb("se_rows", [128, NCH, 128])
        se_n = sb("se_n", [128, NCH, 128])
        se_hi = sb("se_hi", [128, SLOTS], F32R)
        se_lo = sb("se_lo", [128, SLOTS], F32R)
        node_c = sb("node_c", [128, 1])
        weight_c = sb("weight_c", [128, 1])
        weight_pos = sb("weight_pos", [128, 1])
        node_b = sb("node_b", [32, R])
        node_b2 = sb("node_b2", [32, R])
        om_scale = sb("om_scale", [32, R])
        coef = sb("coef", [128, 1])
        coef_pos = sb("coef_pos", [128, 1])
        coef_ln = sb("coef_ln", [128, 1])
        f_bias = sb("f_bias", [128, 1])
        f_low = sb("f_low", [128, 1])
        f_high = sb("f_high", [128, 1])
        omega_f = sb("omega_f", [32, PAIRS, 128])
        omega_st = sb("omega_st", [96, PAIRS, 128], F16)

        xin = sb("xin", [128, 2, TILES, C])
        xres = sb("xres", [128, 2, TILES, C])
        bn6 = sb("bn6", [128, TILES, 6])
        mv = sb("mv", [128, TILES, 2])
        small = sb("small", [128, 16, 64])
        xn = sb("xn", [128, TILES, C])
        junk = sb("junk", [128, NCH, C])
        xg = sb("xg", [128, 2, TILES, C + 1])
        xt_hi = sb("xt_hi", [128, 2, 512], F32R)
        xt_lo = sb("xt_lo", [128, 2, 512], F32R)
        qkv = sb("qkv", [128, TILES, 384])
        qk_sq = sb("qk_sq", [128, TILES, 256])
        qk_n = sb("qk_n", [128, TILES, 256])
        stack = sb("stack", [128, 16, 3, 32], F16)
        stack_t = sb("stack_t", [96, 2, 2, 1024], F16)
        vz = sb("vz", [128, 8, GP, 128])
        feat_e = sb("feat_e", [128, 4, 512])
        qf = sb("qf", [128, 4, 2, T])
        arg = sb("arg", [128, 2, 512])
        s_diag = sb("s_diag", [128, 2, 4, 128])
        s_off = sb("s_off", [128, 2, 2, 128])
        ctx_sb = sb("ctx_sb", [128, 512])
        den = sb("den", [64, 512])
        rden = sb("rden", [64, 512])
        attn_t = sb("attn_t", [128, T])
        maxima = sb("maxima", [128, 6], BF16)
        disp = sb("disp", [128, TILES, SLOTS])
        comb_t = sb("comb_t", [128, NCH, T])
        slot_rs = sb("slot_rs", [128, 2, 2])
        slot_v = sb("slot_v", [128, NCH, 128])
        slot_hi = sb("slot_hi", [128, SLOTS], F32R)
        slot_lo = sb("slot_lo", [128, SLOTS], F32R)
        hid_t = sb("hid_t", [128, MCH, SLOTS])
        proc = sb("proc", [128, NCH, 129])
        comb_rs = sb("comb_rs", [128, TILES])
        ffn_res = sb("ffn_res", [128, TILES, C])
        out_sb = sb("out_sb", [128, 2, TILES, C])

        p_feat = pb("p_feat", [128, 512])
        p_diag = pb("p_diag", [128, 4, 128])
        p_off = pb("p_off", [128, 512])
        p_ctx = pb("p_ctx", [128, 2, 2, 128])
        x01 = pb("x01", [128, 2, 512])
        x23 = pb("x23", [128, 2, 512])
        x2h = x23[:, 0, :].bitcast(F16)
        x3h = x23[:, 1, :].bitcast(F16)

        d_w = sem("d_w")
        d_om = sem("d_om")
        om_zero = sem("om_zero")
        d_x = [sem(f"d_x{u}") for u in range(2)]
        d_out = [sem(f"d_out{u}") for u in range(2)]
        pool_id = sem("pool_id")
        vz_const = sem("vz_const")
        c_dve = sem("c_dve")
        c_act = sem("c_act")
        c_pe = sem("c_pe")
        ln_s = sem("ln_s")
        ln_a = sem("ln_a")
        ln_n = sem("ln_n")
        xn_ok = sem("xn_ok")
        ss_ok = sem("ss_ok")
        ss_cl = sem("ss_cl")
        rms_a = sem("rms_a")
        rms_n = sem("rms_n")
        xg_ok = sem("xg_ok")
        xr_ok = sem("xr_ok")
        tr_ok = sem("tr_ok")
        xth_ok = sem("xth_ok")
        xtl_ok = sem("xtl_ok")
        qkv_ok = sem("qkv_ok")
        qkvs_ok = sem("qkvs_ok")
        sq_ok = sem("sq_ok")
        red_ok = sem("red_ok")
        qk_a = sem("qk_a")
        qk_nw = sem("qk_nw")
        qkn_ok = sem("qkn_ok")
        vz_ok = sem("vz_ok")
        sthi_ok = sem("sthi_ok")
        stlo_ok = sem("stlo_ok")
        stt_ok = sem("stt_ok")
        stq_ok = sem("stq_ok")
        stk_ok = sem("stk_ok")
        ft_ok = sem("ft_ok")
        cl_ok = sem("cl_ok")
        fe_ok = sem("fe_ok")
        qf_ok = sem("qf_ok")
        scd_ok = sem("scd_ok")
        sco_ok = sem("sco_ok")
        sd_ok = sem("sd_ok")
        so_ok = sem("so_ok")
        cx_ok = sem("cx_ok")
        cs_ok = sem("cs_ok")
        den_ok = sem("den_ok")
        at_ok = sem("at_ok")
        wo_ok = sem("wo_ok")
        lg_ok = sem("lg_ok")
        mx_ok = sem("mx_ok")
        sh_ok = sem("sh_ok")
        ed_ok = sem("ed_ok")
        ec_ok = sem("ec_ok")
        sl_ok = sem("sl_ok")
        slr_ok = sem("slr_ok")
        slv_ok = sem("slv_ok")
        slt_ok = sem("slt_ok")
        slh_ok = sem("slh_ok")
        sll_ok = sem("sll_ok")
        hd_ok = sem("hd_ok")
        ge_ok = sem("ge_ok")
        pr_ok = sem("pr_ok")
        prs_ok = sem("prs_ok")
        fi_ok = sem("fi_ok")
        rf_ok = sem("rf_ok")
        o1_ok = sem("o1_ok")
        o2_ok = sem("o2_ok")

        VE, VL, VY, VT, SS, SM, SL, SY, ST_, NQ, NM, NL, NY, NT, CS, CT_ = range(16)

        block = ctx.enter_context(nc.Block())

        @block.sync
        def _(sp):
            def load_x(b, off, w_xn, w_xr):
                after(sp, xn_ok, w_xn)
                after(sp, xr_ok, w_xr)
                sp.dma_start(xin[:, b[1], :, :],
                             x[bass.ds(off, T), :].rearrange("(j p) c -> p j c", p=128)).then_inc(d_x[b[1]], 16)

            def store(b, off, w_o2):
                after(sp, o2_ok, w_o2)
                sp.dma_start(out[bass.ds(off, T), :].rearrange("(j p) c -> p j c", p=128),
                             out_sb[:, b[1], :, :]).then_inc(d_out[b[1]], 16)

            load_x((0, 0), 0, 0, 0)
            load_x((0, 1), T, 0, 0)
            sp.wait_ge(om_zero, 1)
            for hl in range(4):
                for r in range(R):
                    src = omega[r].rearrange("(g q) d m -> q d g m", q=4)[hl]
                    dst = omega_f[8 * hl:8 * hl + 8, :, :].rearrange("d (g u) f -> d g u f", u=2)[
                        :, :, hl // 2, 64 * (hl % 2) + 32 * r:64 * (hl % 2) + 32 * r + 32]
                    sp.dma_start(dst, src).then_inc(d_om, 16)
            sp.dma_start(wqkv_f[:, :], Wqkv).then_inc(d_w, 16)
            sp.dma_start(se_rows[:, :, :], slot_embeds.rearrange("(c p) d -> p c d", p=128)).then_inc(d_w, 16)
            for dst, src, n in ((bqkv_bc, bqkv, 384), (gx_bc, gamma_x, 128), (gs_bc, gamma_slot, 128),
                                (bout_bc, bout, 128)):
                sp.dma_start(dst[:, :], src.rearrange("(a n) -> a n", a=1).broadcast_to([128, n])).then_inc(d_w, 16)
            for q in range(4):
                r = q % 2
                sp.dma_start(node_c[32 * q:32 * q + 32, :],
                             nodes[r:r + 1].rearrange("(a n) -> a n", a=1).broadcast_to([32, 1])).then_inc(d_w, 16)
                sp.dma_start(weight_c[32 * q:32 * q + 32, :],
                             weights[r:r + 1].rearrange("(a n) -> a n", a=1).broadcast_to([32, 1])).then_inc(d_w, 16)
            sp.dma_start(node_b[:, :], nodes.rearrange("(a n) -> a n", a=1).broadcast_to([32, R])).then_inc(d_w, 16)
            sp.dma_start(w1_f[:, :], w1).then_inc(d_w, 16)
            sp.dma_start(w2_sb[:, :, :], w2.rearrange("(c p) d -> p c d", p=128)).then_inc(d_w, 16)
            wv = Wout.rearrange("(g q u d) n -> g u q d n", g=2, q=4, u=2)
            for g in range(GROUPS):
                for u in range(2):
                    for q in range(4):
                        a = 64 * g + 32 * u + 8 * q
                        sp.dma_start(wout_sb[a:a + 8, :], wv[g, u, q]).then_inc(d_w, 16)

            for u in range(2):
                load_x((1, u), (2 + u) * T, 1 + u, 1 + u)
                if u:
                    store((0, 0), 0, 1)
            with sp.Fori(1, B // 2 - 1) as i:
                at_x = [sp.snap(i * (2 * T) + (2 + u) * T) for u in range(2)]
                at_o = [sp.snap(i * (2 * T) + (u - 1) * T) for u in range(2)]
                w_in = [sp.snap(i * 2 + (1 + u)) for u in range(2)]
                w_out = [sp.snap(i * 2 + u) for u in range(2)]
                for u in range(2):
                    load_x((0, u), at_x[u], w_in[u], w_in[u])
                    store((0, 1 - u), at_o[u], w_out[u])
            for b in range(B - 3, B):
                store((0, b % 2), b * T, b + 1)
            for u in range(2):
                sp.wait_ge(d_out[u], 8 * B)

        N_W = 2 + 4 + 8 + 3 + 16

        @block.gpsimd
        def _(pool):
            pool.memset(omega_f[:, :, :], 0.0).then_inc(om_zero, 1)
            pool.memset(ident[:, :], 1.0).then_inc(pool_id, 1)
            pool.memset(causal[:, :], 1.0).then_inc(pool_id, 1)
            pool.wait_ge(pool_id, 2)
            pool.affine_select(out=ident[:, :], in_=ident[:, :], compare_op=ALU.is_equal, fill=0.0, base=0,
                               pattern=[[-1, 128]], channel_multiplier=1).then_inc(pool_id, 1)
            pool.affine_select(out=causal[:, :], in_=causal[:, :], compare_op=ALU.is_ge, fill=0.0, base=0,
                               pattern=[[1, 128]], channel_multiplier=-1).then_inc(pool_id, 1)
            pool.wait_ge(pool_id, 4)
            pool.tensor_copy(ident16[:, :], ident[:, :])
            pool.tensor_scalar(neg_ident[:, :], ident[:, :], -1.0, None, ALU.mult).then_inc(pool_id, 1)
            pool.memset(head_mask[:, :], 1.0).then_inc(pool_id, 1)
            pool.wait_ge(pool_id, 6)
            pool.affine_select(out=head_mask[:, 0:1], in_=head_mask[:, 0:1], compare_op=ALU.is_ge, fill=0.0,
                               base=63, pattern=[[0, 1]], channel_multiplier=-1)
            pool.affine_select(out=head_mask[:, 1:2], in_=head_mask[:, 1:2], compare_op=ALU.is_ge, fill=0.0,
                               base=-64, pattern=[[0, 1]], channel_multiplier=1).then_inc(pool_id, 1)
            pool.wait_ge(pool_id, 7)
            pool.memset(xg[:, :, :, C:C + 1], 1.0)
            pool.memset(proc[:, :, C:C + 1], 1.0)
            pool.memset(vz[:, :, :, :], 0.0).then_inc(vz_const, 1)
            pool.wait_ge(vz_const, 1)
            for q in range(GP):
                pool.memset(vz[:, :, q, 64 + 8 * q:72 + 8 * q], 1.0)
                last = pool.memset(vz[:, :, q, 96 + 8 * q:104 + 8 * q], 1.0)
            last.then_inc(vz_const, 1)
            pool.wait_ge(vz_const, 2)

            def residual(b):
                hold(pool, d_x[b[1]], landed(b, 1))
                hold(pool, o1_ok, count(b, 1, -1))
                pool.tensor_tensor(xres[:, b[1], :, :], xin[:, b[1], :, :],
                                   bout_bc[:, :].rearrange("p (a c) -> p a c", a=1).broadcast_to([128, TILES, C]),
                                   ALU.add).then_inc(xr_ok, 1)

            def squares(b):
                hold(pool, qkvs_ok, count(b, 1, 1))
                pool.tensor_tensor(qk_sq[:, :, :], qkv[:, :, 0:256], qkv[:, :, 0:256], ALU.mult).then_inc(sq_ok, 1)

            def place_v(b):
                hold(pool, qkvs_ok, count(b, 1, 1))
                hold(pool, cx_ok, count(b, 8, -8))
                for j in range(TILES):
                    for q in range(GP):
                        a = 4 * b[1] + 2 * j
                        dst = vz[:, a:a + 2, q, :].rearrange("p g (u c) -> p g u c", c=32)[:, :, 0:2, 8 * q:8 * q + 8]
                        src = qkv[:, j, 256:384].rearrange("p (g q u d) -> p g q u d", g=2, q=4, u=2)[:, :, q]
                        last = pool.tensor_copy(dst, src)
                last.then_inc(vz_ok, 1)

            def place_q(n_b, p):
                hold(pool, fe_ok, count(n_b, 8, p + 1))
                hold(pool, scd_ok, count(n_b, 8, p - 3))
                for h in range(2):
                    last = pool.tensor_scalar(qf[:, p % 4, h, :], feat_e[:, p % 4, 0:T], head_mask[:, h:h + 1],
                                              None, ALU.mult)
                last.then_inc(qf_ok, 1)

            pool.wait_ge(d_w, 16 * N_W)
            residual((0, 0))
            squares((0, 0))
            place_v((0, 0))
            place_q((0, 0), 0)

            def row(b, first, nxt, nxt2):
                b1 = step(b, 1)
                for s in range(8):
                    if s < 7:
                        place_q(b, s + 1)
                    elif nxt:
                        place_q(b1, 0)
                    if s == 1 and nxt:
                        residual(b1)
                    if s == 2 and nxt:
                        squares(b1)
                        place_v(b1)

            run_rows(pool, row)

        @block.scalar
        def _(act):
            def ln_exp(src, log, y, w, done, got):
                nc.scalar.activation(small[:, log, 0:w], small[:, src, 0:w], ACT.Ln).then_inc(done, 1)
                after(act, done, got)
                nc.scalar.activation(small[:, y, 0:w], small[:, log, 0:w], ACT.Exp, scale=-0.5).then_inc(done, 1)

            def ln_root(b):
                after(act, ln_s, count(b, 3, 3))
                ln_exp(VE, VL, VY, 2, ln_a, count(b, 2, 1))

            def sum_squares(b):
                after(act, xn_ok, count(b, 1, 1))
                for j in range(TILES):
                    last = nc.scalar.activation(junk[:, j, :], xn[:, j, :], ACT.Square,
                                                accum_out=small[:, SS, j:j + 1])
                last.then_inc(ss_ok, 1)

            def rms_root(b):
                after(act, ss_cl, count(b, 1, 1))
                ln_exp(SM, SL, SY, 2, rms_a, count(b, 2, 1))

            def xt_high(b):
                after(act, tr_ok, count(b, 1, 1))
                nc.scalar.activation(xt_hi[:, b[1], :], x01[:, 0, :], ACT.Copy).then_inc(xth_ok, 1)

            def qk_root(b):
                after(act, red_ok, count(b, 2, 2))
                ln_exp(NM, NL, NY, 64, qk_a, count(b, 2, 1))

            def stack_high(b):
                after(act, qkn_ok, count(b, 1, 1))
                after(act, stt_ok, count(b, 2, 0))
                for q in (0, 2):
                    last = nc.scalar.activation(stack[:, :, q, :],
                                                qk_n[:, :, :].rearrange("p j (h d) -> p (j h) d", d=32), ACT.Copy)
                last.then_inc(sthi_ok, 1)

            def k_stack(b):
                after(act, stt_ok, count(b, 2, 2))
                nc.scalar.activation(stack_t[:, b[1], 1, :], x3h[0:96, :], ACT.Copy).then_inc(stk_ok, 1)

            def feature_exp(b, p):
                after(act, cl_ok, count(b, 8, p + 1))
                after(act, scd_ok, count(b, 8, p - 3))
                nc.scalar.activation(feat_e[:, p % 4, :], arg[:, p % 2, :], ACT.Exp,
                                     bias=f_bias[:, 0:1]).then_inc(fe_ok, 1)

            def off_copy(b, p):
                after(act, sco_ok, count(b, 8, p + 1))
                after(act, cx_ok, count(b, 8, p - 1))
                nc.scalar.activation(s_off[:, p % 2, :, :], p_off[:, 0:256], ACT.Copy).then_inc(so_ok, 1)

            def ctx_copy(b, g):
                after(act, cx_ok, count(b, 8, 4 * g + 4))
                after(act, at_ok, count(b, 2, g))
                nc.scalar.activation(ctx_sb[:, :], p_ctx[:, :, :, :], ACT.Copy).then_inc(cs_ok, 1)

            def softmax_exps(b):
                after(act, sh_ok, count(b, 2, 1))
                nc.scalar.activation(disp[:, :, :], x01[:, :, :], ACT.Exp).then_inc(ed_ok, 1)
                after(act, sh_ok, count(b, 2, 2))
                nc.scalar.activation(comb_t[:, :, :], x23[:, :, :], ACT.Exp).then_inc(ec_ok, 1)

            def slots_high(b):
                after(act, slt_ok, count(b, 1, 1))
                nc.scalar.activation(slot_hi[:, :], x01[:, 0, :], ACT.Copy).then_inc(slh_ok, 1)

            def gelu(b):
                for half, bank in enumerate((x01, x23)):
                    after(act, hd_ok, count(b, 2, half + 1))
                    nc.scalar.activation(hid_t[:, 2 * half:2 * half + 2, :], bank[:, :, :],
                                         ACT.Gelu).then_inc(ge_ok, 1)

            def proc_copy(b):
                after(act, pr_ok, count(b, 1, 1))
                nc.scalar.activation(proc[:, :, 0:C], x23[:, 1, :], ACT.Copy).then_inc(prs_ok, 1)

            act.wait_ge(c_dve, 2)
            nc.scalar.activation(om_scale[:, :], node_b2[:, :], ACT.Sqrt)
            nc.scalar.activation(coef[:, :], weight_pos[:, :], ACT.Sqrt).then_inc(c_act, 1)
            act.wait_ge(c_dve, 5)
            nc.scalar.activation(coef_ln[:, :], coef_pos[:, :], ACT.Ln).then_inc(c_act, 1)
            act.wait_ge(d_w, 16 * N_W)
            for c in range(NCH):
                last = nc.scalar.activation(junk[:, c, :], se_rows[:, c, :], ACT.Square,
                                            accum_out=small[:, CS, c:c + 1])
            last.then_inc(c_act, 1)
            act.wait_ge(c_dve, 14)
            nc.scalar.activation(small[:, CT_, 4:8], small[:, CT_, 0:4], ACT.Ln).then_inc(c_act, 1)
            act.wait_ge(c_act, 4)
            nc.scalar.activation(small[:, CT_, 8:12], small[:, CT_, 4:8], ACT.Exp, scale=-0.5).then_inc(c_act, 1)
            act.wait_ge(c_pe, 1)
            nc.scalar.activation(se_hi[:, :], x23[:, 0, :], ACT.Copy).then_inc(c_act, 1)

            b0 = (0, 0)
            ln_root(b0)
            sum_squares(b0)
            rms_root(b0)
            xt_high(b0)
            qk_root(b0)
            stack_high(b0)
            k_stack(b0)
            ln_root((0, 1))
            sum_squares((0, 1))
            rms_root((0, 1))
            act.wait_ge(c_dve, 13)
            feature_exp(b0, 0)

            def row(b, first, nxt, nxt2):
                b1, b2, bp = step(b, 1), step(b, 2), step(b, -1)
                for s in range(8):
                    if s < 7:
                        feature_exp(b, s + 1)
                    elif nxt:
                        feature_exp(b1, 0)
                    if s == 1 and nxt:
                        xt_high(b1)
                    if s == 6:
                        slots_high(b)
                        if nxt:
                            k_stack(b1)
                    off_copy(b, s)
                    if s == 0 and not first:
                        ctx_copy(bp, 1)
                    if s == 1 and not first:
                        proc_copy(bp)
                    if s == 4:
                        softmax_exps(b)
                        if nxt:
                            qk_root(b1)
                        if nxt2:
                            ln_root(b2)
                        if nxt:
                            stack_high(b1)
                    if s == 5:
                        ctx_copy(b, 0)
                        if nxt2:
                            sum_squares(b2)
                    if s == 6 and nxt2:
                        rms_root(b2)
                    if s == 7:
                        gelu(b)

            run_rows(act, row)
            last_row = (B // 2 - 1, 1)
            ctx_copy(last_row, 1)
            proc_copy(last_row)

        @block.vector
        def _(dve):
            def newton(src, y, t, w, done, base, extra):
                ys, ts = small[:, y, 0:w], small[:, t, 0:w]
                nc.vector.scalar_tensor_tensor(ts, ys, -0.5, ys, ALU.mult, ALU.mult).then_inc(done, 1)
                after(dve, done, count(base, 3, extra - 2))
                nc.vector.tensor_tensor(ts, ts, small[:, src, 0:w], ALU.mult).then_inc(done, 1)
                after(dve, done, count(base, 3, extra - 1))
                nc.vector.scalar_tensor_tensor(ts, ts, 1.5, ys, ALU.add, ALU.mult).then_inc(done, 1)
                after(dve, done, count(base, 3, extra))

            def ln_stats(b):
                after(dve, d_x[b[1]], landed(b, 1))
                for j in range(TILES):
                    last = nc.vector.bn_stats(bn6[:, j, :], xin[:, b[1], j, :])
                last.then_inc(ln_s, 1)
                hold(dve, ln_s, count(b, 3, 1))
                for j in range(TILES):
                    last = nc.vector.bn_aggr(mv[:, j, :], bn6[:, j, :])
                last.then_inc(ln_s, 1)
                after(dve, ln_s, count(b, 3, 2))
                nc.vector.tensor_scalar(small[:, VE, 0:2], mv[:, :, 1], LN_EPS, None, ALU.add).then_inc(ln_s, 1)

            def ln_apply(b):
                after(dve, ln_a, count(b, 2, 2))
                after(dve, ln_s, count(b, 3, 3))
                newton(VE, VY, VT, 2, ln_n, b, 3)
                after(dve, tr_ok, count(b, 1, 0))
                for j in range(TILES):
                    last = nc.vector.tensor_scalar(xn[:, j, :], xin[:, b[1], j, :], mv[:, j, 0:1],
                                                   small[:, VT, j:j + 1], ALU.subtract, ALU.mult)
                last.then_inc(xn_ok, 1)

            def ss_floor(b):
                after(dve, ss_ok, count(b, 1, 1))
                nc.vector.tensor_scalar(small[:, SM, 0:2], small[:, SS, 0:2], NORM_FLOOR, None,
                                        ALU.max).then_inc(ss_cl, 1)

            def rms_apply(b):
                after(dve, rms_a, count(b, 2, 2))
                after(dve, ss_cl, count(b, 1, 1))
                newton(SM, SY, ST_, 2, rms_n, b, 3)
                after(dve, sl_ok, count(b, 1, -1))
                for j in range(TILES):
                    last = nc.vector.scalar_tensor_tensor(xg[:, b[1], j, 0:C], xn[:, j, :], small[:, ST_, j:j + 1],
                                                          gx_rt[:, :], ALU.mult, ALU.mult)
                last.then_inc(xg_ok, 1)

            def xt_low(b):
                after(dve, xth_ok, count(b, 1, 1))
                nc.vector.tensor_tensor(xt_lo[:, b[1], :], x01[:, 0, :], xt_hi[:, b[1], :].bitcast(F32),
                                        ALU.subtract).then_inc(xtl_ok, 1)

            def qkv_bias(b):
                after(dve, vz_ok, count(b, 1, 0))
                for j in range(TILES):
                    after(dve, qkv_ok, count(b, 2, j + 1))
                    last = nc.vector.tensor_tensor(qkv[:, j, :], x01[:, j, 0:384], bqkv_bc[:, :], ALU.add)
                last.then_inc(qkvs_ok, 1)

            def qk_norms(b):
                after(dve, sq_ok, count(b, 1, 1))
                nc.vector.tensor_reduce(small[:, NQ, :], qk_sq[:, :, :].rearrange("p j (h d) -> p (j h) d", d=HD),
                                        AX_X, ALU.add).then_inc(red_ok, 1)
                after(dve, red_ok, count(b, 2, 1))
                nc.vector.tensor_scalar(small[:, NM, :], small[:, NQ, :], NORM_FLOOR, None,
                                        ALU.max).then_inc(red_ok, 1)

            def qk_apply(b):
                after(dve, qk_a, count(b, 2, 2))
                after(dve, red_ok, count(b, 2, 2))
                newton(NM, NY, NT, 64, qk_nw, b, 3)
                rn = small[:, NT, :].rearrange("p (j h a) -> p j h a", j=2, a=1).broadcast_to([128, 2, 32, HD])
                nc.vector.tensor_tensor(qk_n[:, :, :].rearrange("p j (h d) -> p j h d", d=HD),
                                        qkv[:, :, 0:256].rearrange("p j (h d) -> p j h d", d=HD), rn,
                                        ALU.mult).then_inc(qkn_ok, 1)

            def stack_low(b):
                after(dve, sthi_ok, count(b, 1, 1))
                after(dve, qkn_ok, count(b, 1, 1))
                nc.vector.tensor_tensor(stack[:, :, 1, :], qk_n[:, :, :].rearrange("p j (h d) -> p (j h) d", d=32),
                                        stack[:, :, 0, :], ALU.subtract).then_inc(stlo_ok, 1)

            def q_stack(b):
                after(dve, stt_ok, count(b, 2, 1))
                nc.vector.tensor_copy(stack_t[:, b[1], 0, :], x2h[0:96, :]).then_inc(stq_ok, 1)

            def clip_arg(b, p):
                after(dve, ft_ok, count(b, 8, p + 1))
                after(dve, fe_ok, count(b, 8, p - 1))
                nc.vector.tensor_scalar(arg[:, p % 2, :], p_feat[:, :], f_low[:, 0:1], f_high[:, 0:1], ALU.max,
                                        ALU.min).then_inc(cl_ok, 1)

            def mask(b, p):
                after(dve, scd_ok, count(b, 8, p + 1))
                after(dve, cx_ok, count(b, 8, p - 1))
                nc.vector.tensor_tensor(s_diag[:, p % 2, :, :], p_diag[:, :, :],
                                        causal[:, :].rearrange("p (a t) -> p a t", a=1).broadcast_to([128, 4, 128]),
                                        ALU.mult).then_inc(sd_ok, 1)

            def ctx_norm(b, g):
                after(dve, cs_ok, count(b, 2, g + 1))
                nc.vector.tensor_scalar(den[:, :], ctx_sb[64:128, :], DEN_FLOOR, None, ALU.max).then_inc(den_ok, 1)
                after(dve, den_ok, count(b, 4, 2 * g + 1))
                nc.vector.reciprocal(rden[:, :], den[:, :]).then_inc(den_ok, 1)
                after(dve, den_ok, count(b, 4, 2 * g + 2))
                after(dve, wo_ok, count(b, 1, 0))
                for u in range(2):
                    a = 64 * g + 32 * u
                    last = nc.vector.tensor_tensor(attn_t[a:a + 32, :], ctx_sb[32 * u:32 * u + 32, T * u:T * u + T],
                                                   rden[32 * u:32 * u + 32, T * u:T * u + T], ALU.mult)
                last.then_inc(at_ok, 1)

            def take_maxima(b):
                after(dve, lg_ok, count(b, 2, 1))
                nc.vector.tensor_reduce(maxima[:, 4:6], x01[:, :, :], AX_X, ALU.max)
                after(dve, lg_ok, count(b, 2, 2))
                nc.vector.tensor_reduce(maxima[:, 0:4], x23[:, :, :].rearrange("p a (c t) -> p (a c) t", t=T),
                                        AX_X, ALU.max).then_inc(mx_ok, 1)

            def slots_norm(b):
                after(dve, sl_ok, count(b, 1, 1))
                v = x01[:, :, 0:258].rearrange("p a (c d) -> p a c d", d=129)
                nc.vector.reciprocal(slot_rs[:, :, :], v[:, :, :, C]).then_inc(slr_ok, 1)
                after(dve, slr_ok, count(b, 1, 1))
                rs = slot_rs[:, :, :].rearrange("p a (c d) -> p a c d", d=1).broadcast_to([128, 2, 2, C])
                nc.vector.tensor_tensor(slot_v[:, :, :].rearrange("p (a c) d -> p a c d", a=2), v[:, :, :, 0:C], rs,
                                        ALU.mult).then_inc(slv_ok, 1)

            def slots_low(b):
                after(dve, slh_ok, count(b, 1, 1))
                nc.vector.tensor_tensor(slot_lo[:, :], x01[:, 0, :], slot_hi[:, :].bitcast(F32),
                                        ALU.subtract).then_inc(sll_ok, 1)

            def add_experts(b):
                after(dve, fi_ok, count(b, 1, 1))
                v = x23[:, 0, 0:258].rearrange("p (j d) -> p j d", d=129)
                nc.vector.reciprocal(comb_rs[:, :], v[:, :, C]).then_inc(rf_ok, 1)
                after(dve, rf_ok, count(b, 1, 1))
                after(dve, xr_ok, count(b, 1, 1))
                for j in range(TILES):
                    last = nc.vector.scalar_tensor_tensor(ffn_res[:, j, :], v[:, j, 0:C], comb_rs[:, j:j + 1],
                                                          xres[:, b[1], j, :], ALU.mult, ALU.add)
                last.then_inc(o1_ok, 1)

            def add_attention(b):
                after(dve, wo_ok, count(b, 1, 1))
                after(dve, o1_ok, count(b, 1, 1))
                after(dve, d_out[b[1]], landed(b, 0))
                nc.vector.tensor_tensor(out_sb[:, b[1], :, :],
                                        x23[:, 1, 0:256].rearrange("p (j c) -> p j c", j=2), ffn_res[:, :, :],
                                        ALU.add).then_inc(o2_ok, 1)

            dve.wait_ge(d_w, 16 * N_W)
            nc.vector.tensor_scalar(node_b2[:, :], node_b[:, :], 0.0, 2.0, ALU.max, ALU.mult).then_inc(c_dve, 1)
            nc.vector.tensor_scalar(weight_pos[:, :], weight_c[:, :], 0.0, 1.0 / M, ALU.max, ALU.mult).then_inc(c_dve, 1)
            nc.vector.tensor_scalar(gx_rt[:, :], gx_bc[:, :], float(C) ** 0.5, None, ALU.mult).then_inc(c_dve, 1)
            nc.vector.tensor_scalar(gs_rt[:, :], gs_bc[:, :], float(C) ** 0.5, None, ALU.mult).then_inc(c_dve, 1)
            dve.wait_ge(c_act, 1)
            nc.vector.tensor_scalar(coef_pos[:, :], coef[:, :], 1e-30, None, ALU.max).then_inc(c_dve, 1)
            nc.vector.tensor_scalar(f_low[:, :], node_c[:, :], -CLIP, None, ALU.add).then_inc(c_dve, 1)
            nc.vector.tensor_scalar(f_high[:, :], node_c[:, :], CLIP, None, ALU.add).then_inc(c_dve, 1)
            nc.vector.tensor_copy(wqkv_hi[:, :], wqkv_f[:, :]).then_inc(c_dve, 1)
            nc.vector.tensor_copy(w1_hi[:, :], w1_f[:, :]).then_inc(c_dve, 1)
            dve.wait_ge(c_dve, 9)
            nc.vector.tensor_tensor(wqkv_lo[:, :], wqkv_f[:, :], wqkv_hi[:, :].bitcast(F32), ALU.subtract).then_inc(c_dve, 1)
            nc.vector.tensor_tensor(w1_lo[:, :], w1_f[:, :], w1_hi[:, :].bitcast(F32), ALU.subtract).then_inc(c_dve, 1)
            dve.wait_ge(c_act, 2)
            nc.vector.tensor_tensor(f_bias[:, :], coef_ln[:, :], node_c[:, :], ALU.subtract).then_inc(c_dve, 1)
            dve.wait_ge(d_om, 16 * 8)
            for r in range(R):
                v = omega_f[:, :, :].rearrange("p a (h r m) -> p (a h) r m", h=2, r=R)[:, :, r, :]
                last = nc.vector.tensor_scalar(v, v, om_scale[:, r:r + 1], None, ALU.mult)
            last.then_inc(c_dve, 1)
            dve.wait_ge(c_act, 3)
            nc.vector.tensor_scalar(small[:, CT_, 0:4], small[:, CS, 0:4], NORM_FLOOR, None, ALU.max).then_inc(c_dve, 1)
            dve.wait_ge(c_dve, 14)
            nc.vector.tensor_copy(omega_st[0:32, :, :], omega_f[:, :, :])
            nc.vector.tensor_copy(omega_st[32:64, :, :], omega_f[:, :, :]).then_inc(c_dve, 1)
            dve.wait_ge(c_dve, 15)
            nc.vector.tensor_tensor(omega_st[64:96, :, :], omega_f[:, :, :], omega_st[0:32, :, :],
                                    ALU.subtract).then_inc(c_dve, 1)
            dve.wait_ge(c_act, 5)
            ys, ts = small[:, CT_, 8:12], small[:, CT_, 12:16]
            nc.vector.scalar_tensor_tensor(ts, ys, -0.5, ys, ALU.mult, ALU.mult).then_inc(c_dve, 1)
            dve.wait_ge(c_dve, 17)
            nc.vector.tensor_tensor(ts, ts, small[:, CT_, 0:4], ALU.mult).then_inc(c_dve, 1)
            dve.wait_ge(c_dve, 18)
            nc.vector.scalar_tensor_tensor(ts, ts, 1.5, ys, ALU.add, ALU.mult).then_inc(c_dve, 1)
            dve.wait_ge(c_dve, 19)
            for c in range(NCH):
                last = nc.vector.scalar_tensor_tensor(se_n[:, c, :], se_rows[:, c, :], small[:, CT_, 12 + c:13 + c],
                                                      gs_rt[:, :], ALU.mult, ALU.mult)
            last.then_inc(c_dve, 1)
            dve.wait_ge(c_act, 6)
            nc.vector.tensor_tensor(se_lo[:, :], x23[:, 0, :], se_hi[:, :].bitcast(F32), ALU.subtract).then_inc(c_dve, 1)

            b0 = (0, 0)
            ln_stats(b0)
            ln_apply(b0)
            ss_floor(b0)
            dve.wait_ge(vz_const, 2)
            rms_apply(b0)
            xt_low(b0)
            qkv_bias(b0)
            qk_norms(b0)
            qk_apply(b0)
            stack_low(b0)
            q_stack(b0)
            ln_stats((0, 1))
            ln_apply((0, 1))
            ss_floor((0, 1))
            rms_apply((0, 1))
            clip_arg(b0, 0)

            def row(b, first, nxt, nxt2):
                b1, b2, bp = step(b, 1), step(b, 2), step(b, -1)
                for s in range(8):
                    if s < 7:
                        clip_arg(b, s + 1)
                    elif nxt:
                        clip_arg(b1, 0)
                    if s == 6:
                        slots_low(b)
                        if nxt:
                            q_stack(b1)
                    if s == 1 and nxt:
                        xt_low(b1)
                    mask(b, s)
                    if s == 1 and not first:
                        ctx_norm(bp, 1)
                    if s == 2:
                        if nxt:
                            qkv_bias(b1)
                        if not first:
                            add_experts(bp)
                            add_attention(bp)
                    if s == 3:
                        take_maxima(b)
                        if nxt:
                            qk_norms(b1)
                        if nxt2:
                            ln_stats(b2)
                    if s == 4:
                        if nxt:
                            qk_apply(b1)
                        if nxt2:
                            ln_apply(b2)
                    if s == 5:
                        if nxt:
                            stack_low(b1)
                        slots_norm(b)
                        ctx_norm(b, 0)
                        if nxt2:
                            ss_floor(b2)
                    if s == 6 and nxt2:
                        rms_apply(b2)

            run_rows(dve, row)
            last_row = (B // 2 - 1, 1)
            ctx_norm(last_row, 1)
            add_experts(last_row)
            add_attention(last_row)

        @block.tensor
        def _(pe):
            def three(dst, a_hi, a_lo, w_hi, w_lo, start, stop):
                for i, (a, w) in enumerate(((a_hi, w_hi), (a_hi, w_lo), (a_lo, w_hi))):
                    mm = nc.tensor.matmul(dst, a, w, start=start and i == 0, stop=stop and i == 2,
                                          skip_group_check=True)
                return mm

            def transposes(b):
                after(pe, xg_ok, count(b, 1, 1))
                after(pe, xn_ok, count(b, 1, 1))
                after(pe, ge_ok, count(b, 2, -3))
                for j in range(TILES):
                    nc.tensor.transpose(x01[:, 0, 128 * j:128 * j + 128], xn[:, j, :], ident[:, :])
                for j in range(TILES):
                    mm = nc.tensor.transpose(x01[:, 0, 256 + 128 * j:384 + 128 * j], xg[:, b[1], j, 0:C],
                                             ident[:, :])
                mm.then_inc(tr_ok, 1)

            def qkv_product(b):
                after(pe, xtl_ok, count(b, 1, 1))
                after(pe, xth_ok, count(b, 1, 1))
                for j in range(TILES):
                    sl = slice(128 * j, 128 * j + 128)
                    three(x01[:, j, 0:384], xt_hi[:, b[1], sl], xt_lo[:, b[1], sl], wqkv_hi[:, :], wqkv_lo[:, :],
                          True, True).then_inc(qkv_ok, 1)

            def stacks(b):
                after(pe, stlo_ok, count(b, 1, 1))
                after(pe, sthi_ok, count(b, 1, 1))
                after(pe, ec_ok, count(b, 1, 0))
                for k, bank in enumerate((x2h, x3h)):
                    for g in range(4):
                        for j in range(TILES):
                            mm = nc.tensor.transpose(bank[0:96, 256 * g + 128 * j:256 * g + 128 * j + 128],
                                                     stack[:, 8 * j + 4 * k + g, :, :].rearrange("p a d -> p (a d)"),
                                                     ident16[:, :])
                    mm.then_inc(stt_ok, 1)

            def project(b, p):
                after(pe, stq_ok, count(b, 1, 1))
                after(pe, stk_ok, count(b, 1, 1))
                after(pe, cl_ok, count(b, 8, p))
                g = p // 2
                for k in range(2):
                    mm = nc.tensor.matmul(p_feat[:, T * k:T * k + T], omega_st[:, p, :],
                                          stack_t[:, b[1], k, T * g:T * g + T], start=True, stop=True)
                mm.then_inc(ft_ok, 1)

            def scores(b, p):
                after(pe, qf_ok, count(b, 8, p + 1))
                after(pe, fe_ok, count(b, 8, p + 1))
                after(pe, sd_ok, count(b, 8, p))
                after(pe, so_ok, count(b, 8, p))
                q, k = qf[:, p % 4, :, :], feat_e[:, p % 4, T:2 * T]
                nc.tensor.matmul(p_off[:, 0:256], k[:, 0:128], q[:, :, 128:256], start=True,
                                 stop=True).then_inc(sco_ok, 1)
                nc.tensor.matmul(p_diag[:, 0:2, :], k[:, 0:128], q[:, :, 0:128], start=True, stop=True)
                nc.tensor.matmul(p_diag[:, 2:4, :], k[:, 128:256], q[:, :, 128:256], start=True,
                                 stop=True).then_inc(scd_ok, 1)

            def context(b, p):
                g, q = p // GP, p % GP
                after(pe, sd_ok, count(b, 8, p + 1))
                after(pe, so_ok, count(b, 8, p + 1))
                after(pe, vz_ok, count(b, 1, 1))
                if q == 0:
                    after(pe, cs_ok, count(b, 2, g))
                v0, v1 = vz[:, 4 * b[1] + g, q, :], vz[:, 4 * b[1] + 2 + g, q, :]
                lo, hi = p_ctx[:, :, 0, :], p_ctx[:, :, 1, :]
                nc.tensor.matmul(lo, v0, s_diag[:, p % 2, 0:2, :], start=(q == 0), stop=False, skip_group_check=True)
                nc.tensor.matmul(hi, v0, s_off[:, p % 2, :, :], start=False, stop=False, skip_group_check=True)
                nc.tensor.matmul(hi, v1, s_diag[:, p % 2, 2:4, :], start=False, stop=(q == GP - 1),
                                 skip_group_check=True).then_inc(cx_ok, 1)

            def attention_out(b):
                after(pe, at_ok, count(b, 2, 2))
                after(pe, prs_ok, count(b, 1, 1))
                for j in range(TILES):
                    mm = nc.tensor.matmul(x23[:, 1, 128 * j:128 * j + 128], attn_t[:, 128 * j:128 * j + 128],
                                          wout_sb[:, :], start=True, stop=True)
                mm.then_inc(wo_ok, 1)

            def logits(b, nxt):
                if nxt:
                    after(pe, qkvs_ok, count(b, 1, 2))
                after(pe, ge_ok, count(b, 2, 0))
                after(pe, o1_ok, count(b, 1, 0))
                after(pe, o2_ok, count(b, 1, 0))
                hi, lo = xt_hi[:, b[1], 256:512], xt_lo[:, b[1], 256:512]
                for j in range(TILES):
                    sl = slice(128 * j, 128 * j + 128)
                    mm = three(x01[:, j, :], hi[:, sl], lo[:, sl], se_hi[:, :], se_lo[:, :], True, False)
                mm.then_inc(lg_ok, 1)
                for c in range(NCH):
                    sl = slice(128 * c, 128 * c + 128)
                    mm = three(x23[:, c // 2, T * (c % 2):T * (c % 2) + T], se_hi[:, sl], se_lo[:, sl], hi, lo,
                               c % 2 == 0, False)
                mm.then_inc(lg_ok, 1)

            def shift(b):
                after(pe, mx_ok, count(b, 1, 1))
                for c in range(NCH):
                    for j in range(TILES):
                        mm = nc.tensor.matmul(x01[:, j, 128 * c:128 * c + 128],
                                              maxima[:, c:c + 1].broadcast_to([128, 128]), neg_ident[:, :],
                                              start=False, stop=True, skip_group_check=True)
                mm.then_inc(sh_ok, 1)
                ni = neg_ident[:, :].rearrange("p (a t) -> p a t", a=1).broadcast_to([128, 2, 128])
                for j in range(TILES):
                    for h in range(2):
                        v = x23[:, h, :].rearrange("p (c t) -> p c t", c=2)[:, :, 128 * j:128 * j + 128]
                        mm = nc.tensor.matmul(v, maxima[:, 4 + j:5 + j].broadcast_to([128, 128]), ni,
                                              start=False, stop=True, skip_group_check=True)
                mm.then_inc(sh_ok, 1)

            def slot_sums(b):
                after(pe, ed_ok, count(b, 1, 1))
                for c in range(NCH):
                    for j in range(TILES):
                        mm = nc.tensor.matmul(x01[:, c // 2, 129 * (c % 2):129 * (c % 2) + 129],
                                              disp[:, j, 128 * c:128 * c + 128], xg[:, b[1], j, :],
                                              start=(j == 0), stop=(j == TILES - 1), skip_group_check=True)
                mm.then_inc(sl_ok, 1)

            def slots_transposed(b):
                after(pe, slv_ok, count(b, 1, 1))
                for c in range(NCH):
                    mm = nc.tensor.transpose(x01[:, 0, 128 * c:128 * c + 128], slot_v[:, c, :], ident[:, :])
                mm.then_inc(slt_ok, 1)

            def hidden(b, nxt):
                after(pe, sll_ok, count(b, 1, 1))
                after(pe, slh_ok, count(b, 1, 1))
                if nxt:
                    after(pe, stq_ok, count(b, 1, 2))
                    after(pe, stk_ok, count(b, 1, 2))
                else:
                    after(pe, ec_ok, count(b, 1, 1))
                for m in range(MCH):
                    sl = slice(128 * m, 128 * m + 128)
                    bank = (x01, x23)[m // 2][:, m % 2, :]
                    mm = three(bank, w1_hi[:, sl], w1_lo[:, sl], slot_hi[:, :], slot_lo[:, :], True, True)
                    if m % 2:
                        mm.then_inc(hd_ok, 1)

            def processed(b):
                after(pe, ge_ok, count(b, 2, 2))
                for m in range(MCH):
                    for c in range(NCH):
                        mm = nc.tensor.matmul(x23[:, 1, 128 * c:128 * c + 128], hid_t[:, m, 128 * c:128 * c + 128],
                                              w2_sb[:, m, :], start=(m == 0 and c == 0), stop=(m == MCH - 1),
                                              skip_group_check=True)
                mm.then_inc(pr_ok, 1)

            def combine(b):
                after(pe, prs_ok, count(b, 1, 1))
                after(pe, ec_ok, count(b, 1, 1))
                for j in range(TILES):
                    for c in range(NCH):
                        mm = nc.tensor.matmul(x23[:, 0, 129 * j:129 * j + 129], comb_t[:, c, 128 * j:128 * j + 128],
                                              proc[:, c, :], start=(c == 0), stop=(c == NCH - 1),
                                              skip_group_check=True)
                mm.then_inc(fi_ok, 1)

            pe.wait_ge(pool_id, 5)
            pe.wait_ge(vz_const, 2)
            pe.wait_ge(d_w, 16 * N_W)
            pe.wait_ge(c_dve, 20)
            for c in range(NCH):
                mm = nc.tensor.transpose(x23[:, 0, 128 * c:128 * c + 128], se_n[:, c, :], ident[:, :])
            mm.then_inc(c_pe, 1)
            pe.wait_ge(c_dve, 21)
            b0 = (0, 0)
            transposes(b0)
            qkv_product(b0)
            stacks(b0)
            project(b0, 0)
            project(b0, 1)

            def row(b, first, nxt, nxt2):
                b1, bp = step(b, 1), step(b, -1)
                for s in range(8):
                    scores(b, s)
                    if s > 0:
                        context(b, s - 1)
                    elif not first:
                        context(bp, 7)
                    if s == 0:
                        if nxt:
                            transposes(b1)
                        if not first:
                            processed(bp)
                    if s == 1:
                        if nxt:
                            qkv_product(b1)
                        if not first:
                            combine(bp)
                            attention_out(bp)
                    if s == 2:
                        logits(b, nxt)
                    if s == 3:
                        shift(b)
                    if s == 4:
                        slot_sums(b)
                    if s == 5:
                        if nxt:
                            stacks(b1)
                        slots_transposed(b)
                    if s == 6:
                        hidden(b, nxt)
                    if s < 6:
                        project(b, s + 2)
                    elif nxt:
                        project(b1, s - 6)

            run_rows(pe, row)
            last_row = (B // 2 - 1, 1)
            context(last_row, 7)
            processed(last_row)
            combine(last_row)
            attention_out(last_row)


_INS = ['L0_attn_x', 'L0_attn_Wqkv', 'L0_attn_bqkv', 'L0_attn_Wout', 'L0_attn_bout', 'L0_attn_omega',
        'L0_attn_quad_nodes', 'L0_attn_quad_weights', 'L0_ffn_gamma_x', 'L0_ffn_gamma_slot',
        'L0_ffn_slot_embeds', 'L0_ffn_w1', 'L0_ffn_w2']


def kernel(**inputs):
    import numpy as _np
    import concourse.bacc as _bacc
    from concourse import mybir as _mybir
    from concourse.bass_utils import run_bass_kernel_spmd as _run

    nc = _bacc.Bacc("TRN2", target_bir_lowering=False, num_devices=1)
    shapes = {'L0_attn_x': (B * T, C), 'L0_ffn_slot_embeds': (SLOTS, C)}
    arrays, args = {}, []
    for name in _INS:
        a = _np.ascontiguousarray(inputs[name])
        if name in shapes:
            a = a.reshape(shapes[name])
        arrays[f"in_{name}_dram"] = a
        args.append(nc.dram_tensor(f"in_{name}_dram", a.shape, _mybir.dt.from_np(a.dtype), kind="ExternalInput").ap())
    args.append(nc.dram_tensor("out_0_dram", (B * T, C), _mybir.dt.float32, kind="ExternalOutput").ap())
    build(nc, *args)
    r = _run(nc, [arrays], core_ids=[0])
    return r.results[0]["out_0_dram"].reshape(B, T, C)
```

```python
from contextlib import ExitStack

import concourse.bass as bass
from concourse import mybir

F32 = mybir.dt.float32
F32R = mybir.dt.float32r
F16 = mybir.dt.float16
BF16 = mybir.dt.bfloat16
ALU = mybir.AluOpType
ACT = mybir.ActivationFunctionType
AX_X = mybir.AxisListType.X

B, T, C = 16, 256, 128
HEADS, HD = 16, 8
R, M = 2, 32
PAIRS = HEADS // 2
GROUPS = 2
GP = PAIRS // GROUPS
TILES = T // 128
SLOTS = 512
NCH = SLOTS // 128
HID = 512
MCH = HID // 128
LN_EPS = 1e-5
NORM_FLOOR = 1e-24
DEN_FLOOR = 1e-6
CLIP = 20.0
LN_EXP = "natural_log_exp_and_others"


def count(b, per, extra):
    i, u = b
    if isinstance(i, int):
        return (2 * i + u) * per + extra
    return i * (2 * per) + (u * per + extra)


def landed(b, extra):
    i, u = b
    return i * 16 + 16 * extra


def after(eng, sem, value):
    if isinstance(value, int) and value <= 0:
        return
    eng.wait_ge(sem, value)


def hold(eng, sem, value):
    if isinstance(value, int) and value <= 0:
        return
    eng.wait_ge(sem, value)
    eng.nop(nofuse=True)


def step(b, k):
    i, u = b
    u += k
    return (i + u // 2, u % 2)


def run_rows(eng, row):
    for u in range(2):
        row((0, u), u == 0, True, True)
    with eng.Fori(1, B // 2 - 1) as i:
        for u in range(2):
            row((i, u), False, True, True)
    for u in range(2):
        row((B // 2 - 1, u), False, u == 0, False)


def build(nc, x, Wqkv, bqkv, Wout, bout, omega, nodes, weights, gamma_x, gamma_slot, slot_embeds,
          w1, w2, out):
    with ExitStack() as ctx:
        def sb(name, shape, dt=F32):
            return ctx.enter_context(nc.sbuf_tensor(name, shape, dt))

        def pb(name, shape):
            return ctx.enter_context(nc.psum_tensor(name, shape, F32))

        def sem(name):
            return ctx.enter_context(nc.semaphore(name))

        ident = sb("ident", [128, 128])
        ident16 = sb("ident16", [128, 128], F16)
        neg_ident = sb("neg_ident", [128, 128], BF16)
        causal = sb("causal", [128, 128])
        wqkv_f = sb("wqkv_f", [128, 384])
        wqkv_hi = sb("wqkv_hi", [128, 384], F32R)
        wqkv_lo = sb("wqkv_lo", [128, 384], F32R)
        w1_f = sb("w1_f", [128, HID])
        w1_hi = sb("w1_hi", [128, HID], F32R)
        w1_lo = sb("w1_lo", [128, HID], F32R)
        w2_sb = sb("w2_sb", [128, MCH, 128])
        wout_sb = sb("wout_sb", [128, 128])
        bqkv_bc = sb("bqkv_bc", [128, 384])
        bout_bc = sb("bout_bc", [128, 128])
        gx_bc = sb("gx_bc", [128, 128])
        gs_bc = sb("gs_bc", [128, 128])
        gx_rt = sb("gx_rt", [128, 128])
        gs_rt = sb("gs_rt", [128, 128])
        se_rows = sb("se_rows", [128, NCH, 128])
        se_n = sb("se_n", [128, NCH, 128])
        se_hi = sb("se_hi", [128, SLOTS], F32R)
        se_lo = sb("se_lo", [128, SLOTS], F32R)
        node_c = sb("node_c", [128, 1])
        weight_c = sb("weight_c", [128, 1])
        weight_pos = sb("weight_pos", [128, 1])
        node_b = sb("node_b", [32, R])
        node_b2 = sb("node_b2", [32, R])
        om_scale = sb("om_scale", [32, R])
        coef = sb("coef", [128, 1])
        coef_pos = sb("coef_pos", [128, 1])
        coef_ln = sb("coef_ln", [128, 1])
        f_bias = sb("f_bias", [128, 1])
        f_low = sb("f_low", [128, 1])
        f_high = sb("f_high", [128, 1])
        omega_f = sb("omega_f", [32, PAIRS, 128])
        omega_st = sb("omega_st", [96, PAIRS, 128], F16)

        xin = sb("xin", [128, 2, TILES, C])
        xres = sb("xres", [128, 2, TILES, C])
        bn6 = sb("bn6", [128, TILES, 6])
        mv = sb("mv", [128, TILES, 2])
        small = sb("small", [128, 16, 64])
        xn = sb("xn", [128, TILES, C])
        junk = sb("junk", [128, NCH, C])
        xg = sb("xg", [128, 2, TILES, C + 1])
        xt_hi = sb("xt_hi", [128, 2, 512], F32R)
        xt_lo = sb("xt_lo", [128, 2, 512], F32R)
        qkv = sb("qkv", [128, TILES, 384])
        qk_sq = sb("qk_sq", [128, TILES, 256])
        qk_n = sb("qk_n", [128, TILES, 256])
        stack = sb("stack", [128, 16, 3, 32], F16)
        stack_t = sb("stack_t", [96, 2, 2, 1024], F16)
        vz_hi = sb("vz_hi", [128, 8, GP, 128], F32R)
        vz_lo = sb("vz_lo", [128, 8, GP, 128], F32R)
        kf = sb("kf", [128, 4, T])
        qf = sb("qf", [128, 4, 2, T])
        arg = sb("arg", [128, 2, 512])
        s_mask = sb("s_mask", [128, 2, 4, 128])
        sd_hi = sb("sd_hi", [128, 2, 4, 128], F32R)
        sd_lo = sb("sd_lo", [128, 2, 4, 128], F32R)
        so_hi = sb("so_hi", [128, 2, 2, 128], F32R)
        so_lo = sb("so_lo", [128, 2, 2, 128], F32R)
        ctx_sb = sb("ctx_sb", [128, 512])
        num = sb("num", [128, T])
        den = sb("den", [128, T])
        rden = sb("rden", [128, T])
        attn_t = sb("attn_t", [128, T])
        maxima = sb("maxima", [128, 6], BF16)
        disp = sb("disp", [128, TILES, SLOTS])
        comb_t = sb("comb_t", [128, NCH, T])
        slot_rs = sb("slot_rs", [128, 2, 2])
        slot_v = sb("slot_v", [128, NCH, 128])
        slot_hi = sb("slot_hi", [128, SLOTS], F32R)
        slot_lo = sb("slot_lo", [128, SLOTS], F32R)
        hid_t = sb("hid_t", [128, MCH, SLOTS])
        proc = sb("proc", [128, NCH, 129])
        comb_rs = sb("comb_rs", [128, TILES])
        ffn_res = sb("ffn_res", [128, TILES, C])
        out_sb = sb("out_sb", [128, 2, TILES, C])

        p_feat = pb("p_feat", [128, 512])
        p_diag = pb("p_diag", [128, 4, 128])
        p_off = pb("p_off", [128, 512])
        p_ctx = pb("p_ctx", [128, 2, 2, 128])
        x01 = pb("x01", [128, 2, 512])
        x23 = pb("x23", [128, 2, 512])
        x2h = x23[:, 0, :].bitcast(F16)
        x3h = x23[:, 1, :].bitcast(F16)

        d_qkv = sem("d_qkv")
        d_rows = sem("d_rows")
        d_feat = sem("d_feat")
        d_om = sem("d_om")
        d_se = sem("d_se")
        d_w1 = sem("d_w1")
        d_late = sem("d_late")
        d_bo = sem("d_bo")
        om_zero = sem("om_zero")
        d_x = [sem(f"d_x{u}") for u in range(2)]
        d_out = [sem(f"d_out{u}") for u in range(2)]
        pool_id = sem("pool_id")
        vz_const = sem("vz_const")
        wq_split = sem("wq_split")
        w1_split = sem("w1_split")
        gx_s = sem("gx_s")
        gs_s = sem("gs_s")
        f_in = sem("f_in")
        f_root = sem("f_root")
        f_pos = sem("f_pos")
        f_ln = sem("f_ln")
        f_ok = sem("f_ok")
        om_s = sem("om_s")
        se_ss = sem("se_ss")
        se_cl = sem("se_cl")
        se_a = sem("se_a")
        se_nw = sem("se_nw")
        se_ok = sem("se_ok")
        se_t = sem("se_t")
        se_h = sem("se_h")
        se_l = sem("se_l")
        ln_s = sem("ln_s")
        ln_a = sem("ln_a")
        ln_n = sem("ln_n")
        xn_ok = sem("xn_ok")
        ss_ok = sem("ss_ok")
        ss_cl = sem("ss_cl")
        rms_a = sem("rms_a")
        rms_n = sem("rms_n")
        xg_ok = sem("xg_ok")
        xr_ok = sem("xr_ok")
        tr_ok = sem("tr_ok")
        xth_ok = sem("xth_ok")
        xtl_ok = sem("xtl_ok")
        qkv_ok = sem("qkv_ok")
        qkvs_ok = sem("qkvs_ok")
        sq_ok = sem("sq_ok")
        red_ok = sem("red_ok")
        qk_a = sem("qk_a")
        qk_nw = sem("qk_nw")
        qkn_ok = sem("qkn_ok")
        vzh_ok = sem("vzh_ok")
        vz_ok = sem("vz_ok")
        sthi_ok = sem("sthi_ok")
        stlo_ok = sem("stlo_ok")
        stt_ok = sem("stt_ok")
        stq_ok = sem("stq_ok")
        stk_ok = sem("stk_ok")
        ft_ok = sem("ft_ok")
        cl_ok = sem("cl_ok")
        fe_ok = sem("fe_ok")
        scd_ok = sem("scd_ok")
        sco_ok = sem("sco_ok")
        sm_ok = sem("sm_ok")
        sdh_ok = sem("sdh_ok")
        sdl_ok = sem("sdl_ok")
        soh_ok = sem("soh_ok")
        sol_ok = sem("sol_ok")
        cx_ok = sem("cx_ok")
        cs_ok = sem("cs_ok")
        nd_ok = sem("nd_ok")
        rd_ok = sem("rd_ok")
        at_ok = sem("at_ok")
        wo_ok = sem("wo_ok")
        lg_ok = sem("lg_ok")
        mx_ok = sem("mx_ok")
        sh_ok = sem("sh_ok")
        ed_ok = sem("ed_ok")
        ec_ok = sem("ec_ok")
        sl_ok = sem("sl_ok")
        slr_ok = sem("slr_ok")
        slv_ok = sem("slv_ok")
        slt_ok = sem("slt_ok")
        slh_ok = sem("slh_ok")
        sll_ok = sem("sll_ok")
        hd_ok = sem("hd_ok")
        ge_ok = sem("ge_ok")
        pr_ok = sem("pr_ok")
        prs_ok = sem("prs_ok")
        fi_ok = sem("fi_ok")
        rf_ok = sem("rf_ok")
        o1_ok = sem("o1_ok")
        o2_ok = sem("o2_ok")

        VE, VL, VY, VT, SS, SM, SL, SY, ST_, NQ, NM, NL, NY, NT, CS, CT_ = range(16)

        block = ctx.enter_context(nc.Block())

        @block.sync
        def _(sp):
            def load_x(b, off, w_xn, w_xr):
                after(sp, xn_ok, w_xn)
                after(sp, xr_ok, w_xr)
                sp.dma_start(xin[:, b[1], :, :],
                             x[bass.ds(off, T), :].rearrange("(j p) c -> p j c", p=128)).then_inc(d_x[b[1]], 16)

            def store(b, off, w_o2):
                after(sp, o2_ok, w_o2)
                sp.dma_start(out[bass.ds(off, T), :].rearrange("(j p) c -> p j c", p=128),
                             out_sb[:, b[1], :, :]).then_inc(d_out[b[1]], 16)

            load_x((0, 0), 0, 0, 0)
            sp.dma_start(wqkv_f[:, :], Wqkv).then_inc(d_qkv, 16)
            sp.wait_ge(om_zero, 1)
            for hl in range(4):
                for r in range(R):
                    src = omega[r].rearrange("(g q) d m -> q d g m", q=4)[hl]
                    dst = omega_f[8 * hl:8 * hl + 8, :, :].rearrange("d (g u) f -> d g u f", u=2)[
                        :, :, hl // 2, 64 * (hl % 2) + 32 * r:64 * (hl % 2) + 32 * r + 32]
                    sp.dma_start(dst, src).then_inc(d_om, 16)
            load_x((0, 1), T, 0, 0)
            sp.dma_start(w1_f[:, :], w1).then_inc(d_w1, 16)
            sp.dma_start(w2_sb[:, :, :], w2.rearrange("(c p) d -> p c d", p=128)).then_inc(d_late, 16)
            wv = Wout.rearrange("(g q u d) n -> g u q d n", g=2, q=4, u=2)
            for g in range(GROUPS):
                for u in range(2):
                    a = 64 * g + 32 * u
                    for q in range(4):
                        sp.dma_start(wout_sb[a + 8 * q:a + 8 * q + 8, :], wv[g, u, q]).then_inc(d_late, 16)

            for u in range(2):
                load_x((1, u), (2 + u) * T, 1 + u, 1 + u)
                if u:
                    store((0, 0), 0, 1)
            with sp.Fori(1, B // 2 - 1) as i:
                at_x = [sp.snap(i * (2 * T) + (2 + u) * T) for u in range(2)]
                at_o = [sp.snap(i * (2 * T) + (u - 1) * T) for u in range(2)]
                w_in = [sp.snap(i * 2 + (1 + u)) for u in range(2)]
                w_out = [sp.snap(i * 2 + u) for u in range(2)]
                for u in range(2):
                    load_x((0, u), at_x[u], w_in[u], w_in[u])
                    store((0, 1 - u), at_o[u], w_out[u])
            for b in range(B - 3, B):
                store((0, b % 2), b * T, b + 1)
            for u in range(2):
                sp.wait_ge(d_out[u], 8 * B)

        LATE = 1 + 16

        @block.gpsimd
        def _(pool):
            pool.memset(omega_f[:, :, :], 0.0).then_inc(om_zero, 1)
            pool.memset(ident[:, :], 1.0).then_inc(pool_id, 1)
            pool.memset(causal[:, :], 1.0).then_inc(pool_id, 1)
            pool.wait_ge(pool_id, 2)
            pool.affine_select(out=ident[:, :], in_=ident[:, :], compare_op=ALU.is_equal, fill=0.0, base=0,
                               pattern=[[-1, 128]], channel_multiplier=1).then_inc(pool_id, 1)
            pool.affine_select(out=causal[:, :], in_=causal[:, :], compare_op=ALU.is_ge, fill=0.0, base=0,
                               pattern=[[1, 128]], channel_multiplier=-1).then_inc(pool_id, 1)
            pool.wait_ge(pool_id, 4)
            pool.tensor_copy(ident16[:, :], ident[:, :])
            pool.tensor_scalar(neg_ident[:, :], ident[:, :], -1.0, None, ALU.mult).then_inc(pool_id, 1)
            pool.memset(qf[:, :, :, :], 0.0)
            pool.memset(xg[:, :, :, C:C + 1], 1.0)
            pool.memset(proc[:, :, C:C + 1], 1.0)
            pool.memset(vz_lo[:, :, :, :].bitcast(F32), 0.0)
            pool.memset(vz_hi[:, :, :, :].bitcast(F32), 0.0).then_inc(vz_const, 1)
            pool.wait_ge(vz_const, 1)
            for q in range(GP):
                pool.memset(vz_hi[:, :, q, 64 + 8 * q:72 + 8 * q].bitcast(F32), 1.0)
                last = pool.memset(vz_hi[:, :, q, 96 + 8 * q:104 + 8 * q].bitcast(F32), 1.0)
            last.then_inc(vz_const, 1)
            pool.wait_ge(vz_const, 2)

            def residual(b):
                hold(pool, d_x[b[1]], landed(b, 1))
                hold(pool, o1_ok, count(b, 1, -1))
                pool.tensor_tensor(xres[:, b[1], :, :], xin[:, b[1], :, :],
                                   bout_bc[:, :].rearrange("p (a c) -> p a c", a=1).broadcast_to([128, TILES, C]),
                                   ALU.add).then_inc(xr_ok, 1)

            def squares(b):
                hold(pool, qkvs_ok, count(b, 1, 1))
                pool.tensor_tensor(qk_sq[:, :, :], qkv[:, :, 0:256], qkv[:, :, 0:256], ALU.mult).then_inc(sq_ok, 1)

            def placed(vz, b, j, q):
                a = 4 * b[1] + 2 * j
                return vz[:, a:a + 2, q, :].rearrange("p g (u c) -> p g u c", c=32)[:, :, 0:2, 8 * q:8 * q + 8]

            def v_of(j, q):
                return qkv[:, j, 256:384].rearrange("p (g q u d) -> p g q u d", g=2, q=4, u=2)[:, :, q]

            def place_v_high(b):
                hold(pool, qkvs_ok, count(b, 1, 1))
                hold(pool, cx_ok, count(b, 8, -8))
                for j in range(TILES):
                    for q in range(GP):
                        last = pool.tensor_copy(placed(vz_hi, b, j, q), v_of(j, q))
                last.then_inc(vzh_ok, 1)

            def place_v_low(b):
                hold(pool, vzh_ok, count(b, 1, 1))
                for j in range(TILES):
                    for q in range(GP):
                        last = pool.tensor_tensor(placed(vz_lo, b, j, q), v_of(j, q),
                                                  placed(vz_hi, b, j, q).bitcast(F32), ALU.subtract)
                last.then_inc(vz_ok, 1)

            def qk_apply(b):
                hold(pool, qk_nw, count(b, 3, 3))
                rn = small[:, NT, :].rearrange("p (j h a) -> p j h a", j=2, a=1).broadcast_to([128, 2, 32, HD])
                pool.tensor_tensor(qk_n[:, :, :].rearrange("p j (h d) -> p j h d", d=HD),
                                   qkv[:, :, 0:256].rearrange("p j (h d) -> p j h d", d=HD), rn,
                                   ALU.mult).then_inc(qkn_ok, 1)

            def stack_low(b):
                hold(pool, sthi_ok, count(b, 1, 1))
                hold(pool, qkn_ok, count(b, 1, 1))
                pool.tensor_tensor(stack[:, :, 1, :], qk_n[:, :, :].rearrange("p j (h d) -> p (j h) d", d=32),
                                   stack[:, :, 0, :], ALU.subtract).then_inc(stlo_ok, 1)

            def diag_low(b, p):
                hold(pool, sdh_ok, count(b, 8, p + 1))
                hold(pool, sm_ok, count(b, 8, p + 1))
                hold(pool, cx_ok, count(b, 8, p - 1))
                pool.tensor_tensor(sd_lo[:, p % 2, :, :], s_mask[:, p % 2, :, :],
                                   sd_hi[:, p % 2, :, :].bitcast(F32), ALU.subtract).then_inc(sdl_ok, 1)

            pool.wait_ge(d_bo, 16)
            residual((0, 0))
            squares((0, 0))
            qk_apply((0, 0))
            stack_low((0, 0))
            place_v_high((0, 0))
            place_v_low((0, 0))

            def row(b, first, nxt, nxt2):
                b1 = step(b, 1)
                for s in range(8):
                    if s == 2 and nxt:
                        squares(b1)
                    if s == 4 and nxt:
                        qk_apply(b1)
                    if s == 5 and nxt:
                        stack_low(b1)
                    diag_low(b, s)
                    if s == 2 and nxt:
                        residual(b1)
                        place_v_high(b1)
                    if s == 5 and nxt:
                        place_v_low(b1)

            run_rows(pool, row)

        @block.scalar
        def _(act):
            def ln_exp(src, log, y, w, done, got):
                nc.scalar.activation(small[:, log, 0:w], small[:, src, 0:w], ACT.Ln).then_inc(done, 1)
                after(act, done, got)
                nc.scalar.activation(small[:, y, 0:w], small[:, log, 0:w], ACT.Exp, scale=-0.5).then_inc(done, 1)

            def ln_root(b):
                after(act, ln_s, count(b, 3, 3))
                ln_exp(VE, VL, VY, 2, ln_a, count(b, 2, 1))

            def sum_squares(b):
                after(act, xn_ok, count(b, 1, 1))
                for j in range(TILES):
                    last = nc.scalar.activation(junk[:, j, :], xn[:, j, :], ACT.Square,
                                                accum_out=small[:, SS, j:j + 1])
                last.then_inc(ss_ok, 1)

            def rms_root(b):
                after(act, ss_cl, count(b, 1, 1))
                ln_exp(SM, SL, SY, 2, rms_a, count(b, 2, 1))

            def xt_high(b):
                after(act, tr_ok, count(b, 1, 1))
                nc.scalar.activation(xt_hi[:, b[1], :], x01[:, 0, :], ACT.Copy).then_inc(xth_ok, 1)

            def qk_root(b):
                after(act, red_ok, count(b, 2, 2))
                ln_exp(NM, NL, NY, 64, qk_a, count(b, 2, 1))

            def stack_high(b):
                after(act, qkn_ok, count(b, 1, 1))
                after(act, stt_ok, count(b, 2, 0))
                for q in (0, 2):
                    last = nc.scalar.activation(stack[:, :, q, :],
                                                qk_n[:, :, :].rearrange("p j (h d) -> p (j h) d", d=32), ACT.Copy)
                last.then_inc(sthi_ok, 1)

            def k_stack(b):
                after(act, stt_ok, count(b, 2, 2))
                nc.scalar.activation(stack_t[:, b[1], 1, :], x3h[0:96, :], ACT.Copy).then_inc(stk_ok, 1)

            def feature_exp(b, p):
                after(act, cl_ok, count(b, 8, p + 1))
                after(act, scd_ok, count(b, 8, p - 3))
                nc.scalar.activation(kf[:, p % 4, :], arg[:, p % 2, T:2 * T], ACT.Exp, bias=f_bias[:, 0:1])
                for h in range(2):
                    a = slice(64 * h, 64 * h + 64)
                    last = nc.scalar.activation(qf[a, p % 4, h, :], arg[a, p % 2, 0:T], ACT.Exp, bias=f_bias[a, 0:1])
                last.then_inc(fe_ok, 1)

            def off_high(b, p):
                after(act, sco_ok, count(b, 8, p + 1))
                after(act, cx_ok, count(b, 8, p - 1))
                nc.scalar.activation(so_hi[:, p % 2, :, :], p_off[:, 0:256], ACT.Copy).then_inc(soh_ok, 1)

            def diag_high(b, p):
                after(act, sm_ok, count(b, 8, p + 1))
                after(act, cx_ok, count(b, 8, p - 1))
                nc.scalar.activation(sd_hi[:, p % 2, :, :], s_mask[:, p % 2, :, :], ACT.Copy).then_inc(sdh_ok, 1)

            def ctx_copy(b, g):
                after(act, cx_ok, count(b, 8, 4 * g + 4))
                after(act, nd_ok, count(b, 2, g))
                nc.scalar.activation(ctx_sb[:, :], p_ctx[:, :, :, :], ACT.Copy).then_inc(cs_ok, 1)

            def dispatch_exp(b):
                after(act, sh_ok, count(b, 2, 1))
                nc.scalar.activation(disp[:, :, :], x01[:, :, :], ACT.Exp).then_inc(ed_ok, 1)

            def combine_exp(b):
                after(act, sh_ok, count(b, 2, 2))
                nc.scalar.activation(comb_t[:, :, :], x23[:, :, :], ACT.Exp).then_inc(ec_ok, 1)

            def slots_high(b):
                after(act, slt_ok, count(b, 1, 1))
                nc.scalar.activation(slot_hi[:, :], x01[:, 0, :], ACT.Copy).then_inc(slh_ok, 1)

            def gelu(b):
                for half, bank in enumerate((x01, x23)):
                    after(act, hd_ok, count(b, 2, half + 1))
                    nc.scalar.activation(hid_t[:, 2 * half:2 * half + 2, :], bank[:, :, :],
                                         ACT.Gelu).then_inc(ge_ok, 1)
                nc.scalar.preload_act_table_set(LN_EXP)

            def proc_copy(b):
                after(act, pr_ok, count(b, 1, 1))
                nc.scalar.activation(proc[:, :, 0:C], x23[:, 1, :], ACT.Copy).then_inc(prs_ok, 1)

            def spread(dst, src, n):
                return act.dma_start(dst[:, :], src.rearrange("(a n) -> a n", a=1).broadcast_to([dst.shape[0], n]))

            spread(gx_bc, gamma_x, C).then_inc(d_rows, 16)
            spread(bqkv_bc, bqkv, 3 * C).then_inc(d_rows, 16)
            spread(node_b, nodes, R).then_inc(d_feat, 16)
            for q in range(4):
                r, part = q % R, slice(M * q, M * q + M)
                spread(node_c[part, :], nodes[r:r + 1], 1).then_inc(d_feat, 16)
                spread(weight_c[part, :], weights[r:r + 1], 1).then_inc(d_feat, 16)
            spread(gs_bc, gamma_slot, C).then_inc(d_se, 16)
            act.dma_start(se_rows[:, :, :], slot_embeds.rearrange("(c p) d -> p c d", p=128)).then_inc(d_se, 16)
            spread(bout_bc, bout, C).then_inc(d_bo, 16)

            b0, b1 = (0, 0), (0, 1)
            nc.scalar.preload_act_table_set(LN_EXP)
            ln_root(b0)
            sum_squares(b0)
            rms_root(b0)
            xt_high(b0)
            act.wait_ge(f_in, 1)
            nc.scalar.activation(om_scale[:, :], node_b2[:, :], ACT.Sqrt)
            nc.scalar.activation(coef[:, :], weight_pos[:, :], ACT.Sqrt).then_inc(f_root, 1)
            nc.scalar.preload_act_table_set(LN_EXP)
            act.wait_ge(f_pos, 1)
            nc.scalar.activation(coef_ln[:, :], coef_pos[:, :], ACT.Ln).then_inc(f_ln, 1)
            qk_root(b0)
            stack_high(b0)
            k_stack(b0)
            ln_root(b1)
            sum_squares(b1)
            rms_root(b1)
            act.wait_ge(f_ok, 1)
            act.wait_ge(vz_const, 1)
            feature_exp(b0, 0)
            act.wait_ge(d_se, 32)
            for c in range(NCH):
                last = nc.scalar.activation(junk[:, c, :], se_rows[:, c, :], ACT.Square,
                                            accum_out=small[:, CS, c:c + 1])
            last.then_inc(se_ss, 1)
            act.wait_ge(se_cl, 1)
            nc.scalar.activation(small[:, CT_, 4:8], small[:, CT_, 0:4], ACT.Ln).then_inc(se_a, 1)
            act.wait_ge(se_a, 1)
            nc.scalar.activation(small[:, CT_, 8:12], small[:, CT_, 4:8], ACT.Exp, scale=-0.5).then_inc(se_a, 1)
            act.wait_ge(se_t, 1)
            nc.scalar.activation(se_hi[:, :], x01[:, 0, :], ACT.Copy).then_inc(se_h, 1)

            def row(b, first, nxt, nxt2):
                b1, b2, bp = step(b, 1), step(b, 2), step(b, -1)
                for s in range(8):
                    if s == 1 and nxt:
                        xt_high(b1)
                    if s == 1 and not first:
                        proc_copy(bp)
                    if s == 4:
                        dispatch_exp(b)
                    if s == 5:
                        ctx_copy(b, 0)
                    if s == 6:
                        slots_high(b)
                        if nxt:
                            k_stack(b1)
                    off_high(b, s)
                    if s < 7:
                        feature_exp(b, s + 1)
                    elif nxt:
                        feature_exp(b1, 0)
                    diag_high(b, s)
                    if s == 0 and not first:
                        ctx_copy(bp, 1)
                    if s == 1 and nxt2:
                        ln_root(b2)
                    if s == 2 and nxt:
                        qk_root(b1)
                    if s == 4:
                        combine_exp(b)
                        if nxt:
                            stack_high(b1)
                    if s == 5 and nxt2:
                        sum_squares(b2)
                    if s == 6 and nxt2:
                        rms_root(b2)
                    if s == 7:
                        gelu(b)

            run_rows(act, row)
            last_row = (B // 2 - 1, 1)
            ctx_copy(last_row, 1)
            proc_copy(last_row)

        @block.vector
        def _(dve):
            def newton(src, y, t, w, done, base, extra):
                ys, ts = small[:, y, 0:w], small[:, t, 0:w]
                nc.vector.scalar_tensor_tensor(ts, ys, -0.5, ys, ALU.mult, ALU.mult).then_inc(done, 1)
                after(dve, done, count(base, 3, extra - 2))
                nc.vector.tensor_tensor(ts, ts, small[:, src, 0:w], ALU.mult).then_inc(done, 1)
                after(dve, done, count(base, 3, extra - 1))
                nc.vector.scalar_tensor_tensor(ts, ts, 1.5, ys, ALU.add, ALU.mult).then_inc(done, 1)
                after(dve, done, count(base, 3, extra))

            def ln_stats(b):
                after(dve, d_x[b[1]], landed(b, 1))
                for j in range(TILES):
                    last = nc.vector.bn_stats(bn6[:, j, :], xin[:, b[1], j, :])
                last.then_inc(ln_s, 1)
                hold(dve, ln_s, count(b, 3, 1))
                for j in range(TILES):
                    last = nc.vector.bn_aggr(mv[:, j, :], bn6[:, j, :])
                last.then_inc(ln_s, 1)
                after(dve, ln_s, count(b, 3, 2))
                nc.vector.tensor_scalar(small[:, VE, 0:2], mv[:, :, 1], LN_EPS, None, ALU.add).then_inc(ln_s, 1)

            def ln_apply(b):
                after(dve, ln_a, count(b, 2, 2))
                after(dve, ln_s, count(b, 3, 3))
                newton(VE, VY, VT, 2, ln_n, b, 3)
                after(dve, tr_ok, count(b, 1, 0))
                for j in range(TILES):
                    last = nc.vector.tensor_scalar(xn[:, j, :], xin[:, b[1], j, :], mv[:, j, 0:1],
                                                   small[:, VT, j:j + 1], ALU.subtract, ALU.mult)
                last.then_inc(xn_ok, 1)

            def ss_floor(b):
                after(dve, ss_ok, count(b, 1, 1))
                nc.vector.tensor_scalar(small[:, SM, 0:2], small[:, SS, 0:2], NORM_FLOOR, None,
                                        ALU.max).then_inc(ss_cl, 1)

            def rms_apply(b):
                after(dve, rms_a, count(b, 2, 2))
                after(dve, ss_cl, count(b, 1, 1))
                newton(SM, SY, ST_, 2, rms_n, b, 3)
                after(dve, sl_ok, count(b, 1, -1))
                for j in range(TILES):
                    last = nc.vector.scalar_tensor_tensor(xg[:, b[1], j, 0:C], xn[:, j, :], small[:, ST_, j:j + 1],
                                                          gx_rt[:, :], ALU.mult, ALU.mult)
                last.then_inc(xg_ok, 1)

            def xt_low(b):
                after(dve, xth_ok, count(b, 1, 1))
                nc.vector.tensor_tensor(xt_lo[:, b[1], :], x01[:, 0, :], xt_hi[:, b[1], :].bitcast(F32),
                                        ALU.subtract).then_inc(xtl_ok, 1)

            def qkv_bias(b):
                after(dve, vz_ok, count(b, 1, 0))
                after(dve, qkn_ok, count(b, 1, 0))
                for j in range(TILES):
                    after(dve, qkv_ok, count(b, 2, j + 1))
                    last = nc.vector.tensor_tensor(qkv[:, j, :], x01[:, j, 0:384], bqkv_bc[:, :], ALU.add)
                last.then_inc(qkvs_ok, 1)

            def qk_norms(b):
                after(dve, sq_ok, count(b, 1, 1))
                nc.vector.tensor_reduce(small[:, NQ, :], qk_sq[:, :, :].rearrange("p j (h d) -> p (j h) d", d=HD),
                                        AX_X, ALU.add).then_inc(red_ok, 1)
                after(dve, red_ok, count(b, 2, 1))
                nc.vector.tensor_scalar(small[:, NM, :], small[:, NQ, :], NORM_FLOOR, None,
                                        ALU.max).then_inc(red_ok, 1)

            def qk_newton(b):
                after(dve, qk_a, count(b, 2, 2))
                after(dve, red_ok, count(b, 2, 2))
                newton(NM, NY, NT, 64, qk_nw, b, 3)

            def q_stack(b):
                after(dve, stt_ok, count(b, 2, 1))
                nc.vector.tensor_copy(stack_t[:, b[1], 0, :], x2h[0:96, :]).then_inc(stq_ok, 1)

            def clip_arg(b, p):
                after(dve, ft_ok, count(b, 8, p + 1))
                after(dve, fe_ok, count(b, 8, p - 1))
                nc.vector.tensor_scalar(arg[:, p % 2, :], p_feat[:, :], f_low[:, 0:1], f_high[:, 0:1], ALU.max,
                                        ALU.min).then_inc(cl_ok, 1)

            def mask(b, p):
                after(dve, scd_ok, count(b, 8, p + 1))
                after(dve, sdl_ok, count(b, 8, p - 1))
                nc.vector.tensor_tensor(s_mask[:, p % 2, :, :], p_diag[:, :, :],
                                        causal[:, :].rearrange("p (a t) -> p a t", a=1).broadcast_to([128, 4, 128]),
                                        ALU.mult).then_inc(sm_ok, 1)

            def off_low(b, p):
                after(dve, soh_ok, count(b, 8, p + 1))
                after(dve, cx_ok, count(b, 8, p - 1))
                nc.vector.tensor_tensor(so_lo[:, p % 2, :, :], p_off[:, 0:256],
                                        so_hi[:, p % 2, :, :].bitcast(F32), ALU.subtract).then_inc(sol_ok, 1)

            def ctx_gather(b, g):
                after(dve, cs_ok, count(b, 2, g + 1))
                for u in range(2):
                    a, h = 64 * g + 32 * u, slice(T * u, T * u + T)
                    nc.vector.tensor_copy(num[a:a + 32, :], ctx_sb[32 * u:32 * u + 32, h])
                    last = nc.vector.tensor_scalar(den[a:a + 32, :], ctx_sb[64 + 32 * u:96 + 32 * u, h], DEN_FLOOR,
                                                   None, ALU.max)
                last.then_inc(nd_ok, 1)

            def ctx_norm(b):
                after(dve, nd_ok, count(b, 2, 2))
                nc.vector.reciprocal(rden[:, :], den[:, :]).then_inc(rd_ok, 1)
                after(dve, rd_ok, count(b, 1, 1))
                after(dve, wo_ok, count(b, 1, 0))
                nc.vector.tensor_tensor(attn_t[:, :], num[:, :], rden[:, :], ALU.mult).then_inc(at_ok, 1)

            def token_maxima(b):
                after(dve, lg_ok, count(b, 2, 1))
                nc.vector.tensor_reduce(maxima[:, 4:6], x01[:, :, :], AX_X, ALU.max)

            def slot_maxima(b):
                after(dve, lg_ok, count(b, 2, 2))
                nc.vector.tensor_reduce(maxima[:, 0:4], x23[:, :, :].rearrange("p a (c t) -> p (a c) t", t=T),
                                        AX_X, ALU.max).then_inc(mx_ok, 1)

            def slots_norm(b):
                after(dve, sl_ok, count(b, 1, 1))
                v = x01[:, :, 0:258].rearrange("p a (c d) -> p a c d", d=129)
                nc.vector.reciprocal(slot_rs[:, :, :], v[:, :, :, C]).then_inc(slr_ok, 1)
                after(dve, slr_ok, count(b, 1, 1))
                rs = slot_rs[:, :, :].rearrange("p a (c d) -> p a c d", d=1).broadcast_to([128, 2, 2, C])
                nc.vector.tensor_tensor(slot_v[:, :, :].rearrange("p (a c) d -> p a c d", a=2), v[:, :, :, 0:C], rs,
                                        ALU.mult).then_inc(slv_ok, 1)

            def slots_low(b):
                after(dve, slh_ok, count(b, 1, 1))
                nc.vector.tensor_tensor(slot_lo[:, :], x01[:, 0, :], slot_hi[:, :].bitcast(F32),
                                        ALU.subtract).then_inc(sll_ok, 1)

            def add_experts(b):
                after(dve, fi_ok, count(b, 1, 1))
                v = x23[:, 0, 0:258].rearrange("p (j d) -> p j d", d=129)
                nc.vector.reciprocal(comb_rs[:, :], v[:, :, C]).then_inc(rf_ok, 1)
                after(dve, rf_ok, count(b, 1, 1))
                after(dve, xr_ok, count(b, 1, 1))
                for j in range(TILES):
                    last = nc.vector.scalar_tensor_tensor(ffn_res[:, j, :], v[:, j, 0:C], comb_rs[:, j:j + 1],
                                                          xres[:, b[1], j, :], ALU.mult, ALU.add)
                last.then_inc(o1_ok, 1)

            def add_attention(b):
                after(dve, wo_ok, count(b, 1, 1))
                after(dve, o1_ok, count(b, 1, 1))
                after(dve, d_out[b[1]], landed(b, 0))
                nc.vector.tensor_tensor(out_sb[:, b[1], :, :],
                                        x23[:, 1, 0:256].rearrange("p (j c) -> p j c", j=2), ffn_res[:, :, :],
                                        ALU.add).then_inc(o2_ok, 1)

            b0, b1 = (0, 0), (0, 1)
            ln_stats(b0)
            dve.wait_ge(d_rows, 32)
            nc.vector.tensor_scalar(gx_rt[:, :], gx_bc[:, :], float(C) ** 0.5, None, ALU.mult).then_inc(gx_s, 1)
            ln_apply(b0)
            ss_floor(b0)
            dve.wait_ge(d_qkv, 16)
            nc.vector.tensor_copy(wqkv_hi[:, :], wqkv_f[:, :]).then_inc(wq_split, 1)
            dve.wait_ge(vz_const, 2)
            dve.wait_ge(gx_s, 1)
            rms_apply(b0)
            dve.wait_ge(wq_split, 1)
            nc.vector.tensor_tensor(wqkv_lo[:, :], wqkv_f[:, :], wqkv_hi[:, :].bitcast(F32),
                                    ALU.subtract).then_inc(wq_split, 1)
            xt_low(b0)
            dve.wait_ge(d_feat, 16 * 9)
            nc.vector.tensor_scalar(node_b2[:, :], node_b[:, :], 0.0, 2.0, ALU.max, ALU.mult)
            nc.vector.tensor_scalar(weight_pos[:, :], weight_c[:, :], 0.0, 1.0 / M, ALU.max, ALU.mult).then_inc(f_in, 1)
            nc.vector.tensor_scalar(f_low[:, :], node_c[:, :], -CLIP, None, ALU.add)
            nc.vector.tensor_scalar(f_high[:, :], node_c[:, :], CLIP, None, ALU.add)
            qkv_bias(b0)
            dve.wait_ge(f_root, 1)
            nc.vector.tensor_scalar(coef_pos[:, :], coef[:, :], 1e-30, None, ALU.max).then_inc(f_pos, 1)
            dve.wait_ge(d_om, 16 * 8)
            for r in range(R):
                v = omega_f[:, :, :].rearrange("p a (h r m) -> p (a h) r m", h=2, r=R)[:, :, r, :]
                last = nc.vector.tensor_scalar(v, v, om_scale[:, r:r + 1], None, ALU.mult)
            last.then_inc(om_s, 1)
            qk_norms(b0)
            dve.wait_ge(om_s, 1)
            nc.vector.tensor_copy(omega_st[0:32, :, :], omega_f[:, :, :])
            nc.vector.tensor_copy(omega_st[32:64, :, :], omega_f[:, :, :]).then_inc(om_s, 1)
            dve.wait_ge(om_s, 2)
            nc.vector.tensor_tensor(omega_st[64:96, :, :], omega_f[:, :, :], omega_st[0:32, :, :],
                                    ALU.subtract).then_inc(om_s, 1)
            qk_newton(b0)
            dve.wait_ge(f_ln, 1)
            nc.vector.tensor_tensor(f_bias[:, :], coef_ln[:, :], node_c[:, :], ALU.subtract).then_inc(f_ok, 1)
            q_stack(b0)
            ln_stats(b1)
            ln_apply(b1)
            ss_floor(b1)
            rms_apply(b1)
            dve.wait_ge(f_ok, 1)
            clip_arg(b0, 0)
            dve.wait_ge(d_se, 32)
            nc.vector.tensor_scalar(gs_rt[:, :], gs_bc[:, :], float(C) ** 0.5, None, ALU.mult).then_inc(gs_s, 1)
            dve.wait_ge(d_w1, 16)
            nc.vector.tensor_copy(w1_hi[:, :], w1_f[:, :]).then_inc(w1_split, 1)
            dve.wait_ge(se_ss, 1)
            nc.vector.tensor_scalar(small[:, CT_, 0:4], small[:, CS, 0:4], NORM_FLOOR, None, ALU.max).then_inc(se_cl, 1)
            dve.wait_ge(w1_split, 1)
            nc.vector.tensor_tensor(w1_lo[:, :], w1_f[:, :], w1_hi[:, :].bitcast(F32), ALU.subtract).then_inc(w1_split, 1)
            dve.wait_ge(se_a, 2)
            ys, ts = small[:, CT_, 8:12], small[:, CT_, 12:16]
            nc.vector.scalar_tensor_tensor(ts, ys, -0.5, ys, ALU.mult, ALU.mult).then_inc(se_nw, 1)
            dve.wait_ge(se_nw, 1)
            nc.vector.tensor_tensor(ts, ts, small[:, CT_, 0:4], ALU.mult).then_inc(se_nw, 1)
            dve.wait_ge(se_nw, 2)
            nc.vector.scalar_tensor_tensor(ts, ts, 1.5, ys, ALU.add, ALU.mult).then_inc(se_nw, 1)
            dve.wait_ge(se_nw, 3)
            dve.wait_ge(gs_s, 1)
            for c in range(NCH):
                last = nc.vector.scalar_tensor_tensor(se_n[:, c, :], se_rows[:, c, :], small[:, CT_, 12 + c:13 + c],
                                                      gs_rt[:, :], ALU.mult, ALU.mult)
            last.then_inc(se_ok, 1)
            dve.wait_ge(se_h, 1)
            nc.vector.tensor_tensor(se_lo[:, :], x01[:, 0, :], se_hi[:, :].bitcast(F32), ALU.subtract).then_inc(se_l, 1)

            def row(b, first, nxt, nxt2):
                b1, b2, bp = step(b, 1), step(b, 2), step(b, -1)
                for s in range(8):
                    if s == 1:
                        if not first:
                            ctx_gather(bp, 1)
                        if nxt:
                            xt_low(b1)
                    if s == 2:
                        if nxt:
                            qkv_bias(b1)
                        if not first:
                            add_experts(bp)
                            add_attention(bp)
                    if s == 5:
                        slots_norm(b)
                    if s == 6:
                        slots_low(b)
                        if nxt:
                            q_stack(b1)
                    if s == 3:
                        token_maxima(b)
                    if s < 7:
                        clip_arg(b, s + 1)
                    elif nxt:
                        clip_arg(b1, 0)
                    if s == 3:
                        slot_maxima(b)
                    off_low(b, s)
                    mask(b, s)
                    if s == 0 and nxt2:
                        ln_stats(b2)
                    if s == 1 and not first:
                        ctx_norm(bp)
                    if s == 2 and nxt:
                        qk_norms(b1)
                    if s == 3 and nxt:
                        qk_newton(b1)
                    if s == 4 and nxt2:
                        ln_apply(b2)
                    if s == 5:
                        ctx_gather(b, 0)
                        if nxt2:
                            ss_floor(b2)
                    if s == 7 and nxt2:
                        rms_apply(b2)

            run_rows(dve, row)
            last_row = (B // 2 - 1, 1)
            ctx_gather(last_row, 1)
            ctx_norm(last_row)
            add_experts(last_row)
            add_attention(last_row)

        @block.tensor
        def _(pe):
            def three(dst, a_hi, a_lo, w_hi, w_lo, start, stop):
                for i, (a, w) in enumerate(((a_hi, w_hi), (a_hi, w_lo), (a_lo, w_hi))):
                    mm = nc.tensor.matmul(dst, a, w, start=start and i == 0, stop=stop and i == 2,
                                          skip_group_check=True)
                return mm

            def transposes(b):
                after(pe, xg_ok, count(b, 1, 1))
                after(pe, xn_ok, count(b, 1, 1))
                after(pe, ge_ok, count(b, 2, -3))
                for j in range(TILES):
                    nc.tensor.transpose(x01[:, 0, 128 * j:128 * j + 128], xn[:, j, :], ident[:, :])
                for j in range(TILES):
                    mm = nc.tensor.transpose(x01[:, 0, 256 + 128 * j:384 + 128 * j], xg[:, b[1], j, 0:C],
                                             ident[:, :])
                mm.then_inc(tr_ok, 1)

            def qkv_product(b):
                after(pe, xtl_ok, count(b, 1, 1))
                after(pe, xth_ok, count(b, 1, 1))
                for j in range(TILES):
                    sl = slice(128 * j, 128 * j + 128)
                    three(x01[:, j, 0:384], xt_hi[:, b[1], sl], xt_lo[:, b[1], sl], wqkv_hi[:, :], wqkv_lo[:, :],
                          True, True).then_inc(qkv_ok, 1)

            def stacks(b):
                after(pe, stlo_ok, count(b, 1, 1))
                after(pe, sthi_ok, count(b, 1, 1))
                after(pe, ec_ok, count(b, 1, 0))
                for k, bank in enumerate((x2h, x3h)):
                    for g in range(4):
                        for j in range(TILES):
                            mm = nc.tensor.transpose(bank[0:96, 256 * g + 128 * j:256 * g + 128 * j + 128],
                                                     stack[:, 8 * j + 4 * k + g, :, :].rearrange("p a d -> p (a d)"),
                                                     ident16[:, :])
                    mm.then_inc(stt_ok, 1)

            def project(b, p):
                after(pe, stq_ok, count(b, 1, 1))
                after(pe, stk_ok, count(b, 1, 1))
                after(pe, cl_ok, count(b, 8, p))
                g = p // 2
                for k in range(2):
                    mm = nc.tensor.matmul(p_feat[:, T * k:T * k + T], omega_st[:, p, :],
                                          stack_t[:, b[1], k, T * g:T * g + T], start=True, stop=True)
                mm.then_inc(ft_ok, 1)

            def scores(b, p):
                after(pe, fe_ok, count(b, 8, p + 1))
                after(pe, sm_ok, count(b, 8, p))
                after(pe, soh_ok, count(b, 8, p))
                after(pe, sol_ok, count(b, 8, p))
                q, k = qf[:, p % 4, :, :], kf[:, p % 4, :]
                nc.tensor.matmul(p_off[:, 0:256], k[:, 0:128], q[:, :, 128:256], start=True,
                                 stop=True).then_inc(sco_ok, 1)
                nc.tensor.matmul(p_diag[:, 0:2, :], k[:, 0:128], q[:, :, 0:128], start=True, stop=True)
                nc.tensor.matmul(p_diag[:, 2:4, :], k[:, 128:256], q[:, :, 128:256], start=True,
                                 stop=True).then_inc(scd_ok, 1)

            def context(b, p):
                g, q = p // GP, p % GP
                after(pe, sdh_ok, count(b, 8, p + 1))
                after(pe, sdl_ok, count(b, 8, p + 1))
                after(pe, soh_ok, count(b, 8, p + 1))
                after(pe, sol_ok, count(b, 8, p + 1))
                after(pe, vzh_ok, count(b, 1, 1))
                after(pe, vz_ok, count(b, 1, 1))
                if q == 0:
                    after(pe, cs_ok, count(b, 2, g))
                t0, t1 = 4 * b[1] + g, 4 * b[1] + 2 + g
                lo, hi = p_ctx[:, :, 0, :], p_ctx[:, :, 1, :]
                x = p % 2
                three(lo, vz_hi[:, t0, q, :], vz_lo[:, t0, q, :], sd_hi[:, x, 0:2, :], sd_lo[:, x, 0:2, :], q == 0, False)
                three(hi, vz_hi[:, t0, q, :], vz_lo[:, t0, q, :], so_hi[:, x, :, :], so_lo[:, x, :, :], False, False)
                three(hi, vz_hi[:, t1, q, :], vz_lo[:, t1, q, :], sd_hi[:, x, 2:4, :], sd_lo[:, x, 2:4, :], False,
                    q == GP - 1).then_inc(cx_ok, 1)

            def attention_out(b):
                after(pe, at_ok, count(b, 1, 1))
                after(pe, prs_ok, count(b, 1, 1))
                for j in range(TILES):
                    mm = nc.tensor.matmul(x23[:, 1, 128 * j:128 * j + 128], attn_t[:, 128 * j:128 * j + 128],
                                          wout_sb[:, :], start=True, stop=True)
                mm.then_inc(wo_ok, 1)

            def logits(b, nxt):
                if nxt:
                    after(pe, qkvs_ok, count(b, 1, 2))
                after(pe, ge_ok, count(b, 2, 0))
                after(pe, o1_ok, count(b, 1, 0))
                after(pe, o2_ok, count(b, 1, 0))
                hi, lo = xt_hi[:, b[1], 256:512], xt_lo[:, b[1], 256:512]
                for j in range(TILES):
                    sl = slice(128 * j, 128 * j + 128)
                    mm = three(x01[:, j, :], hi[:, sl], lo[:, sl], se_hi[:, :], se_lo[:, :], True, False)
                mm.then_inc(lg_ok, 1)
                for c in range(NCH):
                    sl = slice(128 * c, 128 * c + 128)
                    mm = three(x23[:, c // 2, T * (c % 2):T * (c % 2) + T], se_hi[:, sl], se_lo[:, sl], hi, lo,
                               c % 2 == 0, False)
                mm.then_inc(lg_ok, 1)

            def shift(b):
                after(pe, mx_ok, count(b, 1, 1))
                for c in range(NCH):
                    for j in range(TILES):
                        mm = nc.tensor.matmul(x01[:, j, 128 * c:128 * c + 128],
                                              maxima[:, c:c + 1].broadcast_to([128, 128]), neg_ident[:, :],
                                              start=False, stop=True, skip_group_check=True)
                mm.then_inc(sh_ok, 1)
                ni = neg_ident[:, :].rearrange("p (a t) -> p a t", a=1).broadcast_to([128, 2, 128])
                for j in range(TILES):
                    for h in range(2):
                        v = x23[:, h, :].rearrange("p (c t) -> p c t", c=2)[:, :, 128 * j:128 * j + 128]
                        mm = nc.tensor.matmul(v, maxima[:, 4 + j:5 + j].broadcast_to([128, 128]), ni,
                                              start=False, stop=True, skip_group_check=True)
                mm.then_inc(sh_ok, 1)

            def slot_sums(b):
                after(pe, ed_ok, count(b, 1, 1))
                for c in range(NCH):
                    for j in range(TILES):
                        mm = nc.tensor.matmul(x01[:, c // 2, 129 * (c % 2):129 * (c % 2) + 129],
                                              disp[:, j, 128 * c:128 * c + 128], xg[:, b[1], j, :],
                                              start=(j == 0), stop=(j == TILES - 1), skip_group_check=True)
                mm.then_inc(sl_ok, 1)

            def slots_transposed(b):
                after(pe, slv_ok, count(b, 1, 1))
                for c in range(NCH):
                    mm = nc.tensor.transpose(x01[:, 0, 128 * c:128 * c + 128], slot_v[:, c, :], ident[:, :])
                mm.then_inc(slt_ok, 1)

            def hidden(b, nxt):
                after(pe, sll_ok, count(b, 1, 1))
                after(pe, slh_ok, count(b, 1, 1))
                if nxt:
                    after(pe, stq_ok, count(b, 1, 2))
                    after(pe, stk_ok, count(b, 1, 2))
                else:
                    after(pe, ec_ok, count(b, 1, 1))
                for m in range(MCH):
                    sl = slice(128 * m, 128 * m + 128)
                    bank = (x01, x23)[m // 2][:, m % 2, :]
                    mm = three(bank, w1_hi[:, sl], w1_lo[:, sl], slot_hi[:, :], slot_lo[:, :], True, True)
                    if m % 2:
                        mm.then_inc(hd_ok, 1)

            def processed(b):
                after(pe, ge_ok, count(b, 2, 2))
                for m in range(MCH):
                    for c in range(NCH):
                        mm = nc.tensor.matmul(x23[:, 1, 128 * c:128 * c + 128], hid_t[:, m, 128 * c:128 * c + 128],
                                              w2_sb[:, m, :], start=(m == 0 and c == 0), stop=(m == MCH - 1),
                                              skip_group_check=True)
                mm.then_inc(pr_ok, 1)

            def combine(b):
                after(pe, prs_ok, count(b, 1, 1))
                after(pe, ec_ok, count(b, 1, 1))
                for j in range(TILES):
                    for c in range(NCH):
                        mm = nc.tensor.matmul(x23[:, 0, 129 * j:129 * j + 129], comb_t[:, c, 128 * j:128 * j + 128],
                                              proc[:, c, :], start=(c == 0), stop=(c == NCH - 1),
                                              skip_group_check=True)
                mm.then_inc(fi_ok, 1)

            b0 = (0, 0)
            pe.wait_ge(pool_id, 5)
            transposes(b0)
            pe.wait_ge(wq_split, 2)
            qkv_product(b0)
            stacks(b0)
            pe.wait_ge(om_s, 3)
            project(b0, 0)
            project(b0, 1)
            pe.wait_ge(se_ok, 1)
            pe.wait_ge(qkvs_ok, 1)
            for c in range(NCH):
                mm = nc.tensor.transpose(x01[:, 0, 128 * c:128 * c + 128], se_n[:, c, :], ident[:, :])
            mm.then_inc(se_t, 1)
            pe.wait_ge(se_l, 1)
            pe.wait_ge(w1_split, 2)
            pe.wait_ge(d_late, 16 * LATE)

            def row(b, first, nxt, nxt2):
                b1, bp = step(b, 1), step(b, -1)
                for s in range(8):
                    scores(b, s)
                    if s > 0:
                        context(b, s - 1)
                    elif not first:
                        context(bp, 7)
                    if s == 0:
                        if nxt:
                            transposes(b1)
                        if not first:
                            processed(bp)
                    if s == 1:
                        if nxt:
                            qkv_product(b1)
                        if not first:
                            combine(bp)
                            attention_out(bp)
                    if s == 2:
                        logits(b, nxt)
                    if s == 3:
                        shift(b)
                    if s == 4:
                        slot_sums(b)
                    if s == 5:
                        if nxt:
                            stacks(b1)
                        slots_transposed(b)
                    if s == 6:
                        hidden(b, nxt)
                    if s < 6:
                        project(b, s + 2)
                    elif nxt:
                        project(b1, s - 6)

            run_rows(pe, row)
            last_row = (B // 2 - 1, 1)
            context(last_row, 7)
            processed(last_row)
            combine(last_row)
            attention_out(last_row)


_INS = ['L0_attn_x', 'L0_attn_Wqkv', 'L0_attn_bqkv', 'L0_attn_Wout', 'L0_attn_bout', 'L0_attn_omega',
        'L0_attn_quad_nodes', 'L0_attn_quad_weights', 'L0_ffn_gamma_x', 'L0_ffn_gamma_slot',
        'L0_ffn_slot_embeds', 'L0_ffn_w1', 'L0_ffn_w2']


def kernel(**inputs):
    import numpy as _np
    import concourse.bacc as _bacc
    from concourse import mybir as _mybir
    from concourse.bass_utils import run_bass_kernel_spmd as _run

    nc = _bacc.Bacc("TRN2", target_bir_lowering=False, num_devices=1)
    shapes = {'L0_attn_x': (B * T, C), 'L0_ffn_slot_embeds': (SLOTS, C)}
    arrays, args = {}, []
    for name in _INS:
        a = _np.ascontiguousarray(inputs[name])
        if name in shapes:
            a = a.reshape(shapes[name])
        arrays[f"in_{name}_dram"] = a
        args.append(nc.dram_tensor(f"in_{name}_dram", a.shape, _mybir.dt.from_np(a.dtype), kind="ExternalInput").ap())
    args.append(nc.dram_tensor("out_0_dram", (B * T, C), _mybir.dt.float32, kind="ExternalOutput").ap())
    build(nc, *args)
    r = _run(nc, [arrays], core_ids=[0])
    return r.results[0]["out_0_dram"].reshape(B, T, C)
```

```python
from contextlib import ExitStack

import concourse.bass as bass
from concourse import mybir

F32 = mybir.dt.float32
F32R = mybir.dt.float32r
F16 = mybir.dt.float16
BF16 = mybir.dt.bfloat16
ALU = mybir.AluOpType
ACT = mybir.ActivationFunctionType
AX_X = mybir.AxisListType.X

B, T, C = 16, 256, 128
HEADS, HD = 16, 8
R, M = 2, 32
PAIRS = HEADS // 2
GROUPS = 4
GP = PAIRS // GROUPS
TILES = T // 128
SLOTS = 512
NCH = SLOTS // 128
HID = 512
MCH = HID // 128
LN_EPS = 1e-5
NORM_FLOOR = 1e-24
DEN_FLOOR = 1e-6
CLIP = 20.0
LN_EXP = "natural_log_exp_and_others"


def count(b, per, extra):
    i, u = b
    if isinstance(i, int):
        return (2 * i + u) * per + extra
    return i * (2 * per) + (u * per + extra)


def landed(b, extra):
    i, u = b
    return i * 16 + 16 * extra


def after(eng, sem, value):
    if isinstance(value, int) and value <= 0:
        return
    eng.wait_ge(sem, value)


def hold(eng, sem, value):
    if isinstance(value, int) and value <= 0:
        return
    eng.wait_ge(sem, value)
    eng.nop(nofuse=True)


def step(b, k):
    i, u = b
    u += k
    return (i + u // 2, u % 2)


def run_rows(eng, row):
    for u in range(2):
        row((0, u), u == 0, True, True)
    with eng.Fori(1, B // 2 - 1) as i:
        for u in range(2):
            row((i, u), False, True, True)
    for u in range(2):
        row((B // 2 - 1, u), False, u == 0, False)


def build(nc, x, Wqkv, bqkv, Wout, bout, omega, nodes, weights, gamma_x, gamma_slot, slot_embeds,
          w1, w2, out):
    with ExitStack() as ctx:
        def sb(name, shape, dt=F32):
            return ctx.enter_context(nc.sbuf_tensor(name, shape, dt))

        def pb(name, shape):
            return ctx.enter_context(nc.psum_tensor(name, shape, F32))

        def sem(name):
            return ctx.enter_context(nc.semaphore(name))

        ident = sb("ident", [128, 128])
        ident16 = sb("ident16", [128, 128], F16)
        neg_ident = sb("neg_ident", [128, 128], BF16)
        causal = sb("causal", [128, 128])
        wqkv_f = sb("wqkv_f", [128, 384])
        wqkv_hi = sb("wqkv_hi", [128, 384], F32R)
        wqkv_lo = sb("wqkv_lo", [128, 384], F32R)
        w1_f = sb("w1_f", [128, HID])
        w1_hi = sb("w1_hi", [128, HID], F32R)
        w1_lo = sb("w1_lo", [128, HID], F32R)
        w2_sb = sb("w2_sb", [128, MCH, 128])
        wout_sb = sb("wout_sb", [128, 2, 128])
        bqkv_bc = sb("bqkv_bc", [128, 384])
        bout_bc = sb("bout_bc", [128, 128])
        gx_bc = sb("gx_bc", [128, 128])
        gs_bc = sb("gs_bc", [128, 128])
        gx_rt = sb("gx_rt", [128, 128])
        gs_rt = sb("gs_rt", [128, 128])
        se_rows = sb("se_rows", [128, NCH, 128])
        se_n = sb("se_n", [128, NCH, 128])
        se_hi = sb("se_hi", [128, SLOTS], F32R)
        se_lo = sb("se_lo", [128, SLOTS], F32R)
        node_c = sb("node_c", [128, 1])
        weight_c = sb("weight_c", [128, 1])
        weight_pos = sb("weight_pos", [128, 1])
        node_b = sb("node_b", [32, R])
        node_b2 = sb("node_b2", [32, R])
        om_scale = sb("om_scale", [32, R])
        coef = sb("coef", [128, 1])
        coef_pos = sb("coef_pos", [128, 1])
        coef_ln = sb("coef_ln", [128, 1])
        f_bias = sb("f_bias", [128, 1])
        f_low = sb("f_low", [128, 1])
        f_high = sb("f_high", [128, 1])
        omega_f = sb("omega_f", [32, PAIRS, 128])
        omega_st = sb("omega_st", [96, PAIRS, 128], F16)

        xin = sb("xin", [128, 2, TILES, C])
        xres = sb("xres", [128, 2, TILES, C])
        bn6 = sb("bn6", [128, TILES, 6])
        mv = sb("mv", [128, TILES, 2])
        small = sb("small", [128, 16, 64])
        xn = sb("xn", [128, TILES, C])
        junk = sb("junk", [128, NCH, C])
        xg = sb("xg", [128, 2, TILES, C + 1])
        xt_hi = sb("xt_hi", [128, 2, 512], F32R)
        xt_lo = sb("xt_lo", [128, 2, 512], F32R)
        qkv = sb("qkv", [128, TILES, 384])
        qk_sq = sb("qk_sq", [128, TILES, 256])
        qk_n = sb("qk_n", [128, TILES, 256])
        stack = sb("stack", [128, 16, 3, 32], F16)
        stack_t = sb("stack_t", [96, 2, 2, 1024], F16)
        vw_all = sb("vw_all", [128, 16, GP, 128], F32R)
        vw_hi = sb("vw_hi", [128, 16, GP, 128], F32R)
        kf = sb("kf", [128, 4, T])
        qf = sb("qf", [128, 4, 2, T])
        arg = sb("arg", [128, 2, 512])
        s_mask = sb("s_mask", [128, 2, 4, 128])
        sd_hi = sb("sd_hi", [128, 2, 4, 128], F32R)
        sd_lo = sb("sd_lo", [128, 2, 4, 128], F32R)
        so_hi = sb("so_hi", [128, 2, 2, 128], F32R)
        so_lo = sb("so_lo", [128, 2, 2, 128], F32R)
        ctx_sb = sb("ctx_sb", [128, 512])
        num = sb("num", [128, 2, T])
        den = sb("den", [128, 2, T])
        rden = sb("rden", [128, 2, T])
        attn_t = sb("attn_t", [128, 2, T])
        maxima = sb("maxima", [128, 6], BF16)
        disp = sb("disp", [128, TILES, SLOTS])
        comb_t = sb("comb_t", [128, NCH, T])
        slot_rs = sb("slot_rs", [128, 2, 2])
        slot_v = sb("slot_v", [128, NCH, 128])
        slot_hi = sb("slot_hi", [128, SLOTS], F32R)
        slot_lo = sb("slot_lo", [128, SLOTS], F32R)
        hid_t = sb("hid_t", [128, MCH, SLOTS])
        proc = sb("proc", [128, NCH, 129])
        comb_rs = sb("comb_rs", [128, TILES])
        ffn_res = sb("ffn_res", [128, TILES, C])
        out_sb = sb("out_sb", [128, 2, TILES, C])

        p_feat = pb("p_feat", [128, 512])
        p_diag = pb("p_diag", [128, 4, 128])
        p_off = pb("p_off", [128, 512])
        p_ctx = pb("p_ctx", [128, 2, 2, 128])
        x01 = pb("x01", [128, 2, 512])
        x23 = pb("x23", [128, 2, 512])
        x2h = x23[:, 0, :].bitcast(F16)
        x3h = x23[:, 1, :].bitcast(F16)

        d_qkv = sem("d_qkv")
        d_rows = sem("d_rows")
        d_feat = sem("d_feat")
        d_om = sem("d_om")
        d_se = sem("d_se")
        d_w1 = sem("d_w1")
        d_late = sem("d_late")
        d_bo = sem("d_bo")
        om_zero = sem("om_zero")
        d_x = [sem(f"d_x{u}") for u in range(2)]
        d_out = [sem(f"d_out{u}") for u in range(2)]
        pool_id = sem("pool_id")
        vz_const = sem("vz_const")
        wq_split = sem("wq_split")
        w1_split = sem("w1_split")
        gx_s = sem("gx_s")
        gs_s = sem("gs_s")
        f_in = sem("f_in")
        f_root = sem("f_root")
        f_pos = sem("f_pos")
        f_ln = sem("f_ln")
        f_ok = sem("f_ok")
        om_s = sem("om_s")
        se_ss = sem("se_ss")
        se_cl = sem("se_cl")
        se_a = sem("se_a")
        se_nw = sem("se_nw")
        se_ok = sem("se_ok")
        se_t = sem("se_t")
        se_h = sem("se_h")
        se_l = sem("se_l")
        ln_s = sem("ln_s")
        ln_a = sem("ln_a")
        ln_n = sem("ln_n")
        xn_ok = sem("xn_ok")
        ss_ok = sem("ss_ok")
        ss_cl = sem("ss_cl")
        rms_a = sem("rms_a")
        rms_n = sem("rms_n")
        xg_ok = sem("xg_ok")
        xr_ok = sem("xr_ok")
        tr_ok = sem("tr_ok")
        xth_ok = sem("xth_ok")
        xtl_ok = sem("xtl_ok")
        qkv_ok = sem("qkv_ok")
        qkvs_ok = sem("qkvs_ok")
        sq_ok = sem("sq_ok")
        red_ok = sem("red_ok")
        qk_a = sem("qk_a")
        qk_nw = sem("qk_nw")
        qkn_ok = sem("qkn_ok")
        vh_ok = sem("vh_ok")
        vl_ok = sem("vl_ok")
        sthi_ok = sem("sthi_ok")
        stlo_ok = sem("stlo_ok")
        stt_ok = sem("stt_ok")
        stq_ok = sem("stq_ok")
        stk_ok = sem("stk_ok")
        ft_ok = sem("ft_ok")
        cl_ok = sem("cl_ok")
        fe_ok = sem("fe_ok")
        scd_ok = sem("scd_ok")
        sco_ok = sem("sco_ok")
        sm_ok = sem("sm_ok")
        sdh_ok = sem("sdh_ok")
        sdl_ok = sem("sdl_ok")
        sdl7_ok = sem("sdl7_ok")
        soh_ok = sem("soh_ok")
        sol_ok = sem("sol_ok")
        cx_ok = sem("cx_ok")
        cs_ok = sem("cs_ok")
        nd_ok = sem("nd_ok")
        rd_ok = sem("rd_ok")
        at_ok = sem("at_ok")
        wo_ok = sem("wo_ok")
        lg_ok = sem("lg_ok")
        mx_ok = sem("mx_ok")
        shd_ok = sem("shd_ok")
        shc_ok = sem("shc_ok")
        ed_ok = sem("ed_ok")
        ec_ok = sem("ec_ok")
        sl_ok = sem("sl_ok")
        slr_ok = sem("slr_ok")
        slv_ok = sem("slv_ok")
        slt_ok = sem("slt_ok")
        slh_ok = sem("slh_ok")
        sll_ok = sem("sll_ok")
        hd_ok = sem("hd_ok")
        ge_ok = sem("ge_ok")
        pr_ok = sem("pr_ok")
        prs_ok = sem("prs_ok")
        fi_ok = sem("fi_ok")
        rf_ok = sem("rf_ok")
        o1_ok = sem("o1_ok")
        o2_ok = sem("o2_ok")

        VE, VL, VY, VT, SS, SM, SL, SY, ST_, NQ, NM, NL, NY, NT, CS, CT_ = range(16)

        block = ctx.enter_context(nc.Block())

        @block.sync
        def _(sp):
            def load_x(b, off, w_xn, w_xr):
                after(sp, xn_ok, w_xn)
                after(sp, xr_ok, w_xr)
                sp.dma_start(xin[:, b[1], :, :],
                             x[bass.ds(off, T), :].rearrange("(j p) c -> p j c", p=128)).then_inc(d_x[b[1]], 16)

            def store(b, off, w_o2):
                after(sp, o2_ok, w_o2)
                sp.dma_start(out[bass.ds(off, T), :].rearrange("(j p) c -> p j c", p=128),
                             out_sb[:, b[1], :, :]).then_inc(d_out[b[1]], 16)

            def spread(dst, src, n):
                return sp.dma_start(dst[:, :], src.rearrange("(a n) -> a n", a=1).broadcast_to([dst.shape[0], n]))

            load_x((0, 0), 0, 0, 0)
            sp.dma_start(wqkv_f[:, :], Wqkv).then_inc(d_qkv, 16)
            spread(node_b, nodes, R).then_inc(d_feat, 16)
            for dst, src in ((node_c, nodes), (weight_c, weights)):
                for h in range(2):
                    sp.dma_start(dst[64 * h:64 * h + 64, :],
                                  src.rearrange("(r m n) -> r m n", m=1, n=1).broadcast_to([R, M, 1])
                                  ).then_inc(d_feat, 16)
            sp.wait_ge(om_zero, 1)
            for hl in range(4):
                for r in range(R):
                    src = omega[r].rearrange("(g q) d m -> q d g m", q=4)[hl]
                    dst = omega_f[8 * hl:8 * hl + 8, :, :].rearrange("d (g u) f -> d g u f", u=2)[
                        :, :, hl // 2, 64 * (hl % 2) + 32 * r:64 * (hl % 2) + 32 * r + 32]
                    sp.dma_start(dst, src).then_inc(d_om, 16)
            load_x((0, 1), T, 0, 0)
            spread(gs_bc, gamma_slot, C).then_inc(d_se, 16)
            sp.dma_start(se_rows[:, :, :], slot_embeds.rearrange("(c p) d -> p c d", p=128)).then_inc(d_se, 16)
            sp.dma_start(w1_f[:, :], w1).then_inc(d_w1, 16)
            spread(bout_bc, bout, C).then_inc(d_bo, 16)
            sp.dma_start(w2_sb[:, :, :], w2.rearrange("(c p) d -> p c d", p=128)).then_inc(d_late, 16)
            wv = Wout.rearrange("(a g q u d) n -> a g u q d n", a=2, g=2, q=GP, u=2)
            for half in range(2):
                for g in range(2):
                    for u in range(2):
                        for hl in range(2):
                            a = 64 * g + 32 * u + 16 * hl
                            sp.dma_start(wout_sb[a:a + 16, half, :], wv[half, g, u]).then_inc(d_late, 16)

            for u in range(2):
                load_x((1, u), (2 + u) * T, 1 + u, 1 + u)
                if u:
                    store((0, 0), 0, 1)
            with sp.Fori(1, B // 2 - 1) as i:
                at_x = [sp.snap(i * (2 * T) + (2 + u) * T) for u in range(2)]
                at_o = [sp.snap(i * (2 * T) + (u - 1) * T) for u in range(2)]
                w_in = [sp.snap(i * 2 + (1 + u)) for u in range(2)]
                w_out = [sp.snap(i * 2 + u) for u in range(2)]
                for u in range(2):
                    load_x((0, u), at_x[u], w_in[u], w_in[u])
                    store((0, 1 - u), at_o[u], w_out[u])
            for b in range(B - 3, B):
                store((0, b % 2), b * T, b + 1)
            for u in range(2):
                sp.wait_ge(d_out[u], 8 * B)

        LATE = 1 + 16

        @block.gpsimd
        def _(pool):
            pool.memset(omega_f[:, :, :], 0.0).then_inc(om_zero, 1)
            pool.memset(ident[:, :], 1.0).then_inc(pool_id, 1)
            pool.memset(causal[:, :], 1.0).then_inc(pool_id, 1)
            pool.wait_ge(pool_id, 2)
            pool.affine_select(out=ident[:, :], in_=ident[:, :], compare_op=ALU.is_equal, fill=0.0, base=0,
                               pattern=[[-1, 128]], channel_multiplier=1).then_inc(pool_id, 1)
            pool.affine_select(out=causal[:, :], in_=causal[:, :], compare_op=ALU.is_ge, fill=0.0, base=0,
                               pattern=[[1, 128]], channel_multiplier=-1).then_inc(pool_id, 1)
            pool.wait_ge(pool_id, 4)
            pool.tensor_copy(ident16[:, :], ident[:, :])
            pool.tensor_scalar(neg_ident[:, :], ident[:, :], -1.0, None, ALU.mult).then_inc(pool_id, 1)
            pool.memset(qf[:, :, :, :], 0.0)
            pool.memset(xg[:, :, :, C:C + 1], 1.0)
            pool.memset(proc[:, :, C:C + 1], 1.0)
            pool.memset(vw_all[:, :, :, :].bitcast(F32), 0.0)
            pool.memset(vw_hi[:, :, :, :].bitcast(F32), 0.0).then_inc(vz_const, 1)
            pool.wait_ge(vz_const, 1)
            for vw in (vw_all, vw_hi):
                for q in range(GP):
                    v = vw[:, :, q, 64:128].bitcast(F32).rearrange("p a (h c) -> p a h c", c=16)
                    last = pool.memset(v[:, :, :, 8 * q:8 * q + 8], 1.0)
            last.then_inc(vz_const, 1)
            pool.wait_ge(vz_const, 2)

            def residual(b):
                hold(pool, d_x[b[1]], landed(b, 1))
                hold(pool, o1_ok, count(b, 1, -1))
                pool.tensor_tensor(xres[:, b[1], :, :], xin[:, b[1], :, :],
                                   bout_bc[:, :].rearrange("p (a c) -> p a c", a=1).broadcast_to([128, TILES, C]),
                                   ALU.add).then_inc(xr_ok, 1)

            def squares(b):
                hold(pool, qkvs_ok, count(b, 1, 1))
                pool.tensor_tensor(qk_sq[:, :, :], qkv[:, :, 0:256], qkv[:, :, 0:256], ALU.mult).then_inc(sq_ok, 1)

            def placed(vw, b, j, q, col):
                a = 8 * b[1] + 4 * j
                v = vw[:, a:a + 4, q, :].rearrange("p g (u c) -> p g u c", c=32)
                return v[:, :, 0:2, col + 8 * q:col + 8 * q + 8]

            def v_of(j, q):
                return qkv[:, j, 256:384].rearrange("p (g q u d) -> p g q u d", g=GROUPS, q=GP, u=2)[:, :, q]

            def place_v_high(b):
                hold(pool, qkvs_ok, count(b, 1, 1))
                hold(pool, cx_ok, count(b, 8, -8))
                for vw in (vw_all, vw_hi):
                    for j in range(TILES):
                        for q in range(GP):
                            last = pool.tensor_copy(placed(vw, b, j, q, 0), v_of(j, q))
                last.then_inc(vh_ok, 1)

            def place_v_low(b):
                hold(pool, vh_ok, count(b, 1, 1))
                for j in range(TILES):
                    for q in range(GP):
                        last = pool.tensor_tensor(placed(vw_all, b, j, q, 16), v_of(j, q),
                                                  placed(vw_all, b, j, q, 0).bitcast(F32), ALU.subtract)
                last.then_inc(vl_ok, 1)

            def qk_apply(b):
                hold(pool, qk_nw, count(b, 3, 3))
                rn = small[:, NT, :].rearrange("p (j h a) -> p j h a", j=2, a=1).broadcast_to([128, 2, 32, HD])
                pool.tensor_tensor(qk_n[:, :, :].rearrange("p j (h d) -> p j h d", d=HD),
                                   qkv[:, :, 0:256].rearrange("p j (h d) -> p j h d", d=HD), rn,
                                   ALU.mult).then_inc(qkn_ok, 1)

            def stack_low(b):
                hold(pool, sthi_ok, count(b, 1, 1))
                hold(pool, qkn_ok, count(b, 1, 1))
                pool.tensor_tensor(stack[:, :, 1, :], qk_n[:, :, :].rearrange("p j (h d) -> p (j h) d", d=32),
                                   stack[:, :, 0, :], ALU.subtract).then_inc(stlo_ok, 1)

            def diag_low(b, p):
                hold(pool, sdh_ok, count(b, 8, p + 1))
                hold(pool, sm_ok, count(b, 8, p + 1))
                hold(pool, cx_ok, count(b, 8, p - 1))
                pool.tensor_tensor(sd_lo[:, p % 2, :, :], s_mask[:, p % 2, :, :],
                                   sd_hi[:, p % 2, :, :].bitcast(F32), ALU.subtract).then_inc(sdl_ok, 1)

            pool.wait_ge(d_bo, 16)
            residual((0, 0))
            squares((0, 0))
            qk_apply((0, 0))
            stack_low((0, 0))
            place_v_high((0, 0))
            place_v_low((0, 0))

            def row(b, first, nxt, nxt2):
                b1 = step(b, 1)
                for s in range(8):
                    if s == 2 and nxt:
                        squares(b1)
                    if s == 4 and nxt:
                        qk_apply(b1)
                    if s == 5 and nxt:
                        stack_low(b1)
                    if s < 7:
                        diag_low(b, s)
                    if s == 2 and nxt:
                        residual(b1)
                        place_v_high(b1)
                    if s == 5 and nxt:
                        place_v_low(b1)

            run_rows(pool, row)

        @block.scalar
        def _(act):
            def ln_exp(src, log, y, w, done, got):
                nc.scalar.activation(small[:, log, 0:w], small[:, src, 0:w], ACT.Ln).then_inc(done, 1)
                after(act, done, got)
                nc.scalar.activation(small[:, y, 0:w], small[:, log, 0:w], ACT.Exp, scale=-0.5).then_inc(done, 1)

            def ln_root(b):
                after(act, ln_s, count(b, 3, 3))
                ln_exp(VE, VL, VY, 2, ln_a, count(b, 2, 1))

            def sum_squares(b):
                after(act, xn_ok, count(b, 1, 1))
                for j in range(TILES):
                    last = nc.scalar.activation(junk[:, j, :], xn[:, j, :], ACT.Square,
                                                accum_out=small[:, SS, j:j + 1])
                last.then_inc(ss_ok, 1)

            def rms_root(b):
                after(act, ss_cl, count(b, 1, 1))
                ln_exp(SM, SL, SY, 2, rms_a, count(b, 2, 1))

            def xt_high(b):
                after(act, tr_ok, count(b, 1, 1))
                nc.scalar.activation(xt_hi[:, b[1], :], x01[:, 0, :], ACT.Copy).then_inc(xth_ok, 1)

            def qk_root(b):
                after(act, red_ok, count(b, 2, 2))
                ln_exp(NM, NL, NY, 64, qk_a, count(b, 2, 1))

            def stack_high(b):
                after(act, qkn_ok, count(b, 1, 1))
                after(act, stt_ok, count(b, 2, 0))
                for q in (0, 2):
                    last = nc.scalar.activation(stack[:, :, q, :],
                                                qk_n[:, :, :].rearrange("p j (h d) -> p (j h) d", d=32), ACT.Copy)
                last.then_inc(sthi_ok, 1)

            def k_stack(b):
                after(act, stt_ok, count(b, 2, 2))
                nc.scalar.activation(stack_t[:, b[1], 1, :], x3h[0:96, :], ACT.Copy).then_inc(stk_ok, 1)

            def feature_exp(b, p):
                after(act, cl_ok, count(b, 8, p + 1))
                after(act, scd_ok, count(b, 8, p - 3))
                nc.scalar.activation(kf[:, p % 4, :], arg[:, p % 2, T:2 * T], ACT.Exp, bias=f_bias[:, 0:1])
                for h in range(2):
                    a = slice(64 * h, 64 * h + 64)
                    last = nc.scalar.activation(qf[a, p % 4, h, :], arg[a, p % 2, 0:T], ACT.Exp, bias=f_bias[a, 0:1])
                last.then_inc(fe_ok, 1)

            def off_high(b, p):
                after(act, sco_ok, count(b, 8, p + 1))
                after(act, cx_ok, count(b, 8, p - 1))
                nc.scalar.activation(so_hi[:, p % 2, :, :], p_off[:, 0:256], ACT.Copy).then_inc(soh_ok, 1)

            def diag_high(b, p):
                after(act, sm_ok, count(b, 8, p + 1))
                after(act, cx_ok, count(b, 8, p - 1))
                nc.scalar.activation(sd_hi[:, p % 2, :, :], s_mask[:, p % 2, :, :], ACT.Copy).then_inc(sdh_ok, 1)

            def ctx_copy(b, g):
                after(act, cx_ok, count(b, 8, GP * g + GP))
                after(act, nd_ok, count(b, GROUPS, g))
                nc.scalar.activation(ctx_sb[:, :], p_ctx[:, :, :, :], ACT.Copy).then_inc(cs_ok, 1)

            def dispatch_exp(b):
                after(act, shd_ok, count(b, 1, 1))
                nc.scalar.activation(disp[:, :, :], x01[:, :, :], ACT.Exp).then_inc(ed_ok, 1)

            def combine_exp(b):
                after(act, shc_ok, count(b, 1, 1))
                nc.scalar.activation(comb_t[:, :, :], x23[:, :, :], ACT.Exp).then_inc(ec_ok, 1)

            def slots_high(b):
                after(act, slt_ok, count(b, 1, 1))
                nc.scalar.activation(slot_hi[:, :], x01[:, 0, :], ACT.Copy).then_inc(slh_ok, 1)

            def gelu(b):
                for half, bank in enumerate((x01, x23)):
                    after(act, hd_ok, count(b, 2, half + 1))
                    nc.scalar.activation(hid_t[:, 2 * half:2 * half + 2, :], bank[:, :, :],
                                         ACT.Gelu).then_inc(ge_ok, 1)

            def proc_copy(b):
                after(act, pr_ok, count(b, 1, 1))
                nc.scalar.activation(proc[:, :, 0:C], x23[:, 1, :], ACT.Copy).then_inc(prs_ok, 1)

            def spread(dst, src, n):
                return act.dma_start(dst[:, :], src.rearrange("(a n) -> a n", a=1).broadcast_to([dst.shape[0], n]))

            spread(gx_bc, gamma_x, C).then_inc(d_rows, 16)
            spread(bqkv_bc, bqkv, 3 * C).then_inc(d_rows, 16)

            b0, b1 = (0, 0), (0, 1)
            nc.scalar.preload_act_table_set(LN_EXP)
            ln_root(b0)
            sum_squares(b0)
            rms_root(b0)
            xt_high(b0)
            act.wait_ge(f_in, 1)
            nc.scalar.activation(om_scale[:, :], node_b2[:, :], ACT.Sqrt)
            nc.scalar.activation(coef[:, :], weight_pos[:, :], ACT.Sqrt).then_inc(f_root, 1)
            nc.scalar.preload_act_table_set(LN_EXP)
            act.wait_ge(f_pos, 1)
            nc.scalar.activation(coef_ln[:, :], coef_pos[:, :], ACT.Ln).then_inc(f_ln, 1)
            qk_root(b0)
            ln_root(b1)
            act.wait_ge(d_se, 32)
            for c in range(NCH):
                last = nc.scalar.activation(junk[:, c, :], se_rows[:, c, :], ACT.Square,
                                            accum_out=small[:, CS, c:c + 1])
            last.then_inc(se_ss, 1)
            stack_high(b0)
            act.wait_ge(se_cl, 1)
            nc.scalar.activation(small[:, CT_, 4:8], small[:, CT_, 0:4], ACT.Ln).then_inc(se_a, 1)
            act.wait_ge(se_a, 1)
            nc.scalar.activation(small[:, CT_, 8:12], small[:, CT_, 4:8], ACT.Exp, scale=-0.5).then_inc(se_a, 1)
            sum_squares(b1)
            k_stack(b0)
            rms_root(b1)
            act.wait_ge(se_t, 1)
            nc.scalar.activation(se_hi[:, :], x01[:, 0, :], ACT.Copy).then_inc(se_h, 1)
            act.wait_ge(f_ok, 1)
            act.wait_ge(vz_const, 1)
            feature_exp(b0, 0)

            def row(b, first, nxt, nxt2):
                b1, b2, bp = step(b, 1), step(b, 2), step(b, -1)
                for s in range(8):
                    if s == 1 and not first:
                        proc_copy(bp)
                    if s == 4:
                        dispatch_exp(b)
                    if s == 3:
                        ctx_copy(b, 0)
                    if s == 7:
                        ctx_copy(b, 2)
                    if s == 6:
                        slots_high(b)
                        if nxt:
                            k_stack(b1)
                    if s == 7 and not nxt:
                        gelu(b)
                    off_high(b, s)
                    if s == 6 and nxt2:
                        sum_squares(b2)
                    if s < 7:
                        feature_exp(b, s + 1)
                    elif nxt:
                        feature_exp(b1, 0)
                    if s == 0:
                        if not first:
                            ctx_copy(bp, 3)
                        if nxt:
                            xt_high(b1)
                    diag_high(b, s)
                    if s == 2 and nxt:
                        qk_root(b1)
                    if s == 4:
                        if nxt:
                            stack_high(b1)
                        combine_exp(b)
                        ctx_copy(b, 1)
                        if nxt2:
                            ln_root(b2)
                    if s == 6 and nxt2:
                        rms_root(b2)
                    if s == 7 and nxt:
                        gelu(b)
                        nc.scalar.preload_act_table_set(LN_EXP)

            run_rows(act, row)
            last_row = (B // 2 - 1, 1)
            proc_copy(last_row)
            ctx_copy(last_row, 3)

        @block.vector
        def _(dve):
            def newton(src, y, t, w, done, base, extra):
                ys, ts = small[:, y, 0:w], small[:, t, 0:w]
                nc.vector.scalar_tensor_tensor(ts, ys, -0.5, ys, ALU.mult, ALU.mult).then_inc(done, 1)
                after(dve, done, count(base, 3, extra - 2))
                nc.vector.tensor_tensor(ts, ts, small[:, src, 0:w], ALU.mult).then_inc(done, 1)
                after(dve, done, count(base, 3, extra - 1))
                nc.vector.scalar_tensor_tensor(ts, ts, 1.5, ys, ALU.add, ALU.mult).then_inc(done, 1)
                after(dve, done, count(base, 3, extra))

            def ln_stats(b):
                after(dve, d_x[b[1]], landed(b, 1))
                for j in range(TILES):
                    last = nc.vector.bn_stats(bn6[:, j, :], xin[:, b[1], j, :])
                last.then_inc(ln_s, 1)
                hold(dve, ln_s, count(b, 3, 1))
                for j in range(TILES):
                    last = nc.vector.bn_aggr(mv[:, j, :], bn6[:, j, :])
                last.then_inc(ln_s, 1)
                after(dve, ln_s, count(b, 3, 2))
                nc.vector.tensor_scalar(small[:, VE, 0:2], mv[:, :, 1], LN_EPS, None, ALU.add).then_inc(ln_s, 1)

            def ln_apply(b):
                after(dve, ln_a, count(b, 2, 2))
                after(dve, ln_s, count(b, 3, 3))
                newton(VE, VY, VT, 2, ln_n, b, 3)
                after(dve, tr_ok, count(b, 1, 0))
                for j in range(TILES):
                    last = nc.vector.tensor_scalar(xn[:, j, :], xin[:, b[1], j, :], mv[:, j, 0:1],
                                                   small[:, VT, j:j + 1], ALU.subtract, ALU.mult)
                last.then_inc(xn_ok, 1)

            def ss_floor(b):
                after(dve, ss_ok, count(b, 1, 1))
                nc.vector.tensor_scalar(small[:, SM, 0:2], small[:, SS, 0:2], NORM_FLOOR, None,
                                        ALU.max).then_inc(ss_cl, 1)

            def rms_apply(b):
                after(dve, rms_a, count(b, 2, 2))
                after(dve, ss_cl, count(b, 1, 1))
                newton(SM, SY, ST_, 2, rms_n, b, 3)
                after(dve, sl_ok, count(b, 1, -1))
                for j in range(TILES):
                    last = nc.vector.scalar_tensor_tensor(xg[:, b[1], j, 0:C], xn[:, j, :], small[:, ST_, j:j + 1],
                                                          gx_rt[:, :], ALU.mult, ALU.mult)
                last.then_inc(xg_ok, 1)

            def xt_low(b):
                after(dve, xth_ok, count(b, 1, 1))
                nc.vector.tensor_tensor(xt_lo[:, b[1], :], x01[:, 0, :], xt_hi[:, b[1], :].bitcast(F32),
                                        ALU.subtract).then_inc(xtl_ok, 1)

            def qkv_bias(b):
                after(dve, vl_ok, count(b, 1, 0))
                after(dve, qkn_ok, count(b, 1, 0))
                for j in range(TILES):
                    after(dve, qkv_ok, count(b, 2, j + 1))
                    last = nc.vector.tensor_tensor(qkv[:, j, :], x01[:, j, 0:384], bqkv_bc[:, :], ALU.add)
                last.then_inc(qkvs_ok, 1)

            def qk_norms(b):
                after(dve, sq_ok, count(b, 1, 1))
                nc.vector.tensor_reduce(small[:, NQ, :], qk_sq[:, :, :].rearrange("p j (h d) -> p (j h) d", d=HD),
                                        AX_X, ALU.add).then_inc(red_ok, 1)
                after(dve, red_ok, count(b, 2, 1))
                nc.vector.tensor_scalar(small[:, NM, :], small[:, NQ, :], NORM_FLOOR, None,
                                        ALU.max).then_inc(red_ok, 1)

            def qk_newton(b):
                after(dve, qk_a, count(b, 2, 2))
                after(dve, red_ok, count(b, 2, 2))
                newton(NM, NY, NT, 64, qk_nw, b, 3)

            def q_stack(b):
                after(dve, stt_ok, count(b, 2, 1))
                nc.vector.tensor_copy(stack_t[:, b[1], 0, :], x2h[0:96, :]).then_inc(stq_ok, 1)

            def clip_arg(b, p):
                after(dve, ft_ok, count(b, 8, p + 1))
                after(dve, fe_ok, count(b, 8, p - 1))
                nc.vector.tensor_scalar(arg[:, p % 2, :], p_feat[:, :], f_low[:, 0:1], f_high[:, 0:1], ALU.max,
                                        ALU.min).then_inc(cl_ok, 1)

            def mask(b, p):
                after(dve, scd_ok, count(b, 8, p + 1))
                if p == 1:
                    after(dve, sdl7_ok, count(b, 1, 0))
                else:
                    after(dve, sdl_ok, count(b, 7, p - 1))
                nc.vector.tensor_tensor(s_mask[:, p % 2, :, :], p_diag[:, :, :],
                                        causal[:, :].rearrange("p (a t) -> p a t", a=1).broadcast_to([128, 4, 128]),
                                        ALU.mult).then_inc(sm_ok, 1)

            def last_diag_low(b):
                after(dve, sdh_ok, count(b, 8, 8))
                after(dve, sm_ok, count(b, 8, 8))
                after(dve, cx_ok, count(b, 8, 6))
                nc.vector.tensor_tensor(sd_lo[:, 1, :, :], s_mask[:, 1, :, :], sd_hi[:, 1, :, :].bitcast(F32),
                                        ALU.subtract).then_inc(sdl7_ok, 1)

            def off_low(b, p):
                after(dve, soh_ok, count(b, 8, p + 1))
                after(dve, cx_ok, count(b, 8, p - 1))
                nc.vector.tensor_tensor(so_lo[:, p % 2, :, :], p_off[:, 0:256],
                                        so_hi[:, p % 2, :, :].bitcast(F32), ALU.subtract).then_inc(sol_ok, 1)

            def ctx_gather(b, g):
                after(dve, cs_ok, count(b, GROUPS, g + 1))
                after(dve, at_ok, count(b, 2, g // 2 - 1))
                for u in range(2):
                    a, h = 64 * (g % 2) + 32 * u, slice(T * u, T * u + T)
                    nc.vector.tensor_copy(num[a:a + 32, g // 2, :], ctx_sb[32 * u:32 * u + 32, h])
                    last = nc.vector.tensor_scalar(den[a:a + 32, g // 2, :], ctx_sb[64 + 32 * u:96 + 32 * u, h],
                                                   DEN_FLOOR, None, ALU.max)
                last.then_inc(nd_ok, 1)

            def ctx_norm(b, half):
                after(dve, nd_ok, count(b, GROUPS, 2 * half + 2))
                nc.vector.reciprocal(rden[:, half, :], den[:, half, :]).then_inc(rd_ok, 1)
                after(dve, rd_ok, count(b, 2, half + 1))
                after(dve, wo_ok, count(b, 1, 0))
                nc.vector.tensor_tensor(attn_t[:, half, :], num[:, half, :], rden[:, half, :],
                                        ALU.mult).then_inc(at_ok, 1)

            def token_maxima(b):
                after(dve, lg_ok, count(b, 2, 1))
                nc.vector.tensor_reduce(maxima[:, 4:6], x01[:, :, :], AX_X, ALU.max)

            def slot_maxima(b):
                after(dve, lg_ok, count(b, 2, 2))
                nc.vector.tensor_reduce(maxima[:, 0:4], x23[:, :, :].rearrange("p a (c t) -> p (a c) t", t=T),
                                        AX_X, ALU.max).then_inc(mx_ok, 1)

            def slots_norm(b):
                after(dve, sl_ok, count(b, 1, 1))
                v = x01[:, :, 0:258].rearrange("p a (c d) -> p a c d", d=129)
                nc.vector.reciprocal(slot_rs[:, :, :], v[:, :, :, C]).then_inc(slr_ok, 1)
                after(dve, slr_ok, count(b, 1, 1))
                rs = slot_rs[:, :, :].rearrange("p a (c d) -> p a c d", d=1).broadcast_to([128, 2, 2, C])
                nc.vector.tensor_tensor(slot_v[:, :, :].rearrange("p (a c) d -> p a c d", a=2), v[:, :, :, 0:C], rs,
                                        ALU.mult).then_inc(slv_ok, 1)

            def slots_low(b):
                after(dve, slh_ok, count(b, 1, 1))
                nc.vector.tensor_tensor(slot_lo[:, :], x01[:, 0, :], slot_hi[:, :].bitcast(F32),
                                        ALU.subtract).then_inc(sll_ok, 1)

            def add_experts(b):
                after(dve, fi_ok, count(b, 1, 1))
                v = x23[:, 0, 0:258].rearrange("p (j d) -> p j d", d=129)
                nc.vector.reciprocal(comb_rs[:, :], v[:, :, C]).then_inc(rf_ok, 1)
                after(dve, rf_ok, count(b, 1, 1))
                after(dve, xr_ok, count(b, 1, 1))
                for j in range(TILES):
                    last = nc.vector.scalar_tensor_tensor(ffn_res[:, j, :], v[:, j, 0:C], comb_rs[:, j:j + 1],
                                                          xres[:, b[1], j, :], ALU.mult, ALU.add)
                last.then_inc(o1_ok, 1)

            def add_attention(b):
                after(dve, wo_ok, count(b, 1, 1))
                after(dve, o1_ok, count(b, 1, 1))
                after(dve, d_out[b[1]], landed(b, 0))
                nc.vector.tensor_tensor(out_sb[:, b[1], :, :],
                                        x23[:, 1, 0:256].rearrange("p (j c) -> p j c", j=2), ffn_res[:, :, :],
                                        ALU.add).then_inc(o2_ok, 1)

            b0, b1 = (0, 0), (0, 1)
            ln_stats(b0)
            dve.wait_ge(d_rows, 32)
            nc.vector.tensor_scalar(gx_rt[:, :], gx_bc[:, :], float(C) ** 0.5, None, ALU.mult).then_inc(gx_s, 1)
            ln_apply(b0)
            ss_floor(b0)
            dve.wait_ge(d_qkv, 16)
            nc.vector.tensor_copy(wqkv_hi[:, :], wqkv_f[:, :]).then_inc(wq_split, 1)
            dve.wait_ge(gx_s, 1)
            rms_apply(b0)
            dve.wait_ge(wq_split, 1)
            nc.vector.tensor_tensor(wqkv_lo[:, :], wqkv_f[:, :], wqkv_hi[:, :].bitcast(F32),
                                    ALU.subtract).then_inc(wq_split, 1)
            xt_low(b0)
            dve.wait_ge(d_feat, 16 * 5)
            nc.vector.tensor_scalar(node_b2[:, :], node_b[:, :], 0.0, 2.0, ALU.max, ALU.mult)
            nc.vector.tensor_scalar(weight_pos[:, :], weight_c[:, :], 0.0, 1.0 / M, ALU.max, ALU.mult).then_inc(f_in, 1)
            nc.vector.tensor_scalar(f_low[:, :], node_c[:, :], -CLIP, None, ALU.add)
            nc.vector.tensor_scalar(f_high[:, :], node_c[:, :], CLIP, None, ALU.add)
            qkv_bias(b0)
            dve.wait_ge(f_root, 1)
            nc.vector.tensor_scalar(coef_pos[:, :], coef[:, :], 1e-30, None, ALU.max).then_inc(f_pos, 1)
            dve.wait_ge(d_om, 16 * 8)
            for r in range(R):
                v = omega_f[:, :, :].rearrange("p a (h r m) -> p (a h) r m", h=2, r=R)[:, :, r, :]
                last = nc.vector.tensor_scalar(v, v, om_scale[:, r:r + 1], None, ALU.mult)
            last.then_inc(om_s, 1)
            qk_norms(b0)
            ln_stats(b1)
            qk_newton(b0)
            dve.wait_ge(om_s, 1)
            nc.vector.tensor_copy(omega_st[0:32, :, :], omega_f[:, :, :])
            nc.vector.tensor_copy(omega_st[32:64, :, :], omega_f[:, :, :]).then_inc(om_s, 1)
            dve.wait_ge(om_s, 2)
            nc.vector.tensor_tensor(omega_st[64:96, :, :], omega_f[:, :, :], omega_st[0:32, :, :],
                                    ALU.subtract).then_inc(om_s, 1)
            dve.wait_ge(f_ln, 1)
            nc.vector.tensor_tensor(f_bias[:, :], coef_ln[:, :], node_c[:, :], ALU.subtract).then_inc(f_ok, 1)
            dve.wait_ge(d_se, 32)
            nc.vector.tensor_scalar(gs_rt[:, :], gs_bc[:, :], float(C) ** 0.5, None, ALU.mult).then_inc(gs_s, 1)
            dve.wait_ge(se_ss, 1)
            nc.vector.tensor_scalar(small[:, CT_, 0:4], small[:, CS, 0:4], NORM_FLOOR, None, ALU.max).then_inc(se_cl, 1)
            ln_apply(b1)
            dve.wait_ge(se_a, 2)
            ys, ts = small[:, CT_, 8:12], small[:, CT_, 12:16]
            nc.vector.scalar_tensor_tensor(ts, ys, -0.5, ys, ALU.mult, ALU.mult).then_inc(se_nw, 1)
            dve.wait_ge(se_nw, 1)
            nc.vector.tensor_tensor(ts, ts, small[:, CT_, 0:4], ALU.mult).then_inc(se_nw, 1)
            dve.wait_ge(se_nw, 2)
            nc.vector.scalar_tensor_tensor(ts, ts, 1.5, ys, ALU.add, ALU.mult).then_inc(se_nw, 1)
            dve.wait_ge(se_nw, 3)
            dve.wait_ge(gs_s, 1)
            for c in range(NCH):
                last = nc.vector.scalar_tensor_tensor(se_n[:, c, :], se_rows[:, c, :], small[:, CT_, 12 + c:13 + c],
                                                      gs_rt[:, :], ALU.mult, ALU.mult)
            last.then_inc(se_ok, 1)
            q_stack(b0)
            ss_floor(b1)
            clip_arg(b0, 0)
            dve.wait_ge(se_h, 1)
            nc.vector.tensor_tensor(se_lo[:, :], x01[:, 0, :], se_hi[:, :].bitcast(F32), ALU.subtract).then_inc(se_l, 1)
            rms_apply(b1)
            dve.wait_ge(d_w1, 16)
            nc.vector.tensor_copy(w1_hi[:, :], w1_f[:, :]).then_inc(w1_split, 1)
            dve.wait_ge(w1_split, 1)
            nc.vector.tensor_tensor(w1_lo[:, :], w1_f[:, :], w1_hi[:, :].bitcast(F32), ALU.subtract).then_inc(w1_split, 1)

            def row(b, first, nxt, nxt2):
                b1, b2, bp = step(b, 1), step(b, 2), step(b, -1)
                for s in range(8):
                    if s == 1:
                        if not first:
                            ctx_gather(bp, 3)
                        if nxt:
                            xt_low(b1)
                    if s == 2:
                        if nxt:
                            qkv_bias(b1)
                        if not first:
                            add_experts(bp)
                            add_attention(bp)
                    if s == 5:
                        slots_norm(b)
                    if s == 6:
                        slots_low(b)
                        if nxt:
                            q_stack(b1)
                    if s == 3:
                        token_maxima(b)
                    if s < 7:
                        clip_arg(b, s + 1)
                    elif nxt:
                        clip_arg(b1, 0)
                    if s == 3:
                        slot_maxima(b)
                    if s == 0 and not first:
                        ctx_norm(bp, 0)
                    off_low(b, s)
                    mask(b, s)
                    if s == 1 and not first:
                        ctx_norm(bp, 1)
                    if s == 2 and nxt:
                        qk_norms(b1)
                    if s == 3 and nxt:
                        qk_newton(b1)
                    if s == 4:
                        ctx_gather(b, 0)
                        if nxt2:
                            ln_stats(b2)
                    if s == 5:
                        ctx_gather(b, 1)
                        if nxt2:
                            ln_apply(b2)
                    if s == 6 and nxt2:
                        ss_floor(b2)
                    if s == 7:
                        last_diag_low(b)
                        if nxt2:
                            rms_apply(b2)
                        ctx_gather(b, 2)

            run_rows(dve, row)
            last_row = (B // 2 - 1, 1)
            ctx_norm(last_row, 0)
            ctx_gather(last_row, 3)
            ctx_norm(last_row, 1)
            add_experts(last_row)
            add_attention(last_row)

        @block.tensor
        def _(pe):
            def three(dst, a_hi, a_lo, w_hi, w_lo, start, stop):
                for i, (a, w) in enumerate(((a_hi, w_hi), (a_hi, w_lo), (a_lo, w_hi))):
                    mm = nc.tensor.matmul(dst, a, w, start=start and i == 0, stop=stop and i == 2,
                                          skip_group_check=True)
                return mm

            def transposes(b):
                after(pe, xg_ok, count(b, 1, 1))
                after(pe, xn_ok, count(b, 1, 1))
                after(pe, ge_ok, count(b, 2, -3))
                for j in range(TILES):
                    nc.tensor.transpose(x01[:, 0, 128 * j:128 * j + 128], xn[:, j, :], ident[:, :])
                for j in range(TILES):
                    mm = nc.tensor.transpose(x01[:, 0, 256 + 128 * j:384 + 128 * j], xg[:, b[1], j, 0:C],
                                             ident[:, :])
                mm.then_inc(tr_ok, 1)

            def qkv_product(b):
                after(pe, xtl_ok, count(b, 1, 1))
                after(pe, xth_ok, count(b, 1, 1))
                for j in range(TILES):
                    sl = slice(128 * j, 128 * j + 128)
                    three(x01[:, j, 0:384], xt_hi[:, b[1], sl], xt_lo[:, b[1], sl], wqkv_hi[:, :], wqkv_lo[:, :],
                          True, True).then_inc(qkv_ok, 1)

            def stacks(b):
                after(pe, stlo_ok, count(b, 1, 1))
                after(pe, sthi_ok, count(b, 1, 1))
                after(pe, ec_ok, count(b, 1, 0))
                for k, bank in enumerate((x2h, x3h)):
                    for g in range(4):
                        for j in range(TILES):
                            mm = nc.tensor.transpose(bank[0:96, 256 * g + 128 * j:256 * g + 128 * j + 128],
                                                     stack[:, 8 * j + 4 * k + g, :, :].rearrange("p a d -> p (a d)"),
                                                     ident16[:, :])
                    mm.then_inc(stt_ok, 1)

            def project(b, p):
                after(pe, stq_ok, count(b, 1, 1))
                after(pe, stk_ok, count(b, 1, 1))
                after(pe, cl_ok, count(b, 8, p))
                g = p // 2
                for k in range(2):
                    mm = nc.tensor.matmul(p_feat[:, T * k:T * k + T], omega_st[:, p, :],
                                          stack_t[:, b[1], k, T * g:T * g + T], start=True, stop=True)
                mm.then_inc(ft_ok, 1)

            def scores(b, p):
                after(pe, fe_ok, count(b, 8, p + 1))
                after(pe, sm_ok, count(b, 8, p))
                after(pe, soh_ok, count(b, 8, p))
                after(pe, sol_ok, count(b, 8, p))
                q, k = qf[:, p % 4, :, :], kf[:, p % 4, :]
                nc.tensor.matmul(p_off[:, 0:256], k[:, 0:128], q[:, :, 128:256], start=True,
                                 stop=True).then_inc(sco_ok, 1)
                nc.tensor.matmul(p_diag[:, 0:2, :], k[:, 0:128], q[:, :, 0:128], start=True, stop=True)
                nc.tensor.matmul(p_diag[:, 2:4, :], k[:, 128:256], q[:, :, 128:256], start=True,
                                 stop=True).then_inc(scd_ok, 1)

            def context(b, p):
                g, q, x = p // GP, p % GP, p % 2
                after(pe, sdh_ok, count(b, 8, p + 1))
                if p < 7:
                    after(pe, sdl_ok, count(b, 7, p + 1))
                else:
                    after(pe, sdl7_ok, count(b, 1, 1))
                after(pe, soh_ok, count(b, 8, p + 1))
                after(pe, sol_ok, count(b, 8, p + 1))
                after(pe, vh_ok, count(b, 1, 1))
                after(pe, vl_ok, count(b, 1, 1))
                if q == 0:
                    after(pe, cs_ok, count(b, GROUPS, g))
                t0, t1 = 8 * b[1] + g, 8 * b[1] + 4 + g
                lo, hi = p_ctx[:, :, 0, :], p_ctx[:, :, 1, :]
                products = ((lo, t0, sd_hi[:, x, 0:2, :], sd_lo[:, x, 0:2, :]),
                            (hi, t0, so_hi[:, x, :, :], so_lo[:, x, :, :]),
                            (hi, t1, sd_hi[:, x, 2:4, :], sd_lo[:, x, 2:4, :]))
                for i, (dst, t, s_hi, s_lo) in enumerate(products):
                    nc.tensor.matmul(dst, vw_all[:, t, q, :], s_hi, start=(q == 0 and i == 0), stop=False,
                                     skip_group_check=True)
                    mm = nc.tensor.matmul(dst, vw_hi[:, t, q, :], s_lo, start=False, stop=(q == GP - 1 and i != 1),
                                          skip_group_check=True)
                mm.then_inc(cx_ok, 1)

            def attention_out(b):
                after(pe, prs_ok, count(b, 1, 1))
                for half in range(2):
                    after(pe, at_ok, count(b, 2, half + 1))
                    for j in range(TILES):
                        mm = nc.tensor.matmul(x23[:, 1, 128 * j:128 * j + 128],
                                              attn_t[:, half, 128 * j:128 * j + 128], wout_sb[:, half, :],
                                              start=(half == 0 and j == 0), stop=(half == 1), skip_group_check=True)
                mm.then_inc(wo_ok, 1)

            def logits(b, nxt):
                if nxt:
                    after(pe, qkvs_ok, count(b, 1, 2))
                after(pe, ge_ok, count(b, 2, 0))
                after(pe, o1_ok, count(b, 1, 0))
                after(pe, o2_ok, count(b, 1, 0))
                hi, lo = xt_hi[:, b[1], 256:512], xt_lo[:, b[1], 256:512]
                for j in range(TILES):
                    sl = slice(128 * j, 128 * j + 128)
                    mm = three(x01[:, j, :], hi[:, sl], lo[:, sl], se_hi[:, :], se_lo[:, :], True, False)
                mm.then_inc(lg_ok, 1)
                for c in range(NCH):
                    sl = slice(128 * c, 128 * c + 128)
                    mm = three(x23[:, c // 2, T * (c % 2):T * (c % 2) + T], se_hi[:, sl], se_lo[:, sl], hi, lo,
                               c % 2 == 0, False)
                mm.then_inc(lg_ok, 1)

            def shift(b):
                after(pe, mx_ok, count(b, 1, 1))
                for c in range(NCH):
                    for j in range(TILES):
                        mm = nc.tensor.matmul(x01[:, j, 128 * c:128 * c + 128],
                                              maxima[:, c:c + 1].broadcast_to([128, 128]), neg_ident[:, :],
                                              start=False, stop=True, skip_group_check=True)
                mm.then_inc(shd_ok, 1)
                ni = neg_ident[:, :].rearrange("p (a t) -> p a t", a=1).broadcast_to([128, 2, 128])
                for j in range(TILES):
                    for h in range(2):
                        v = x23[:, h, :].rearrange("p (c t) -> p c t", c=2)[:, :, 128 * j:128 * j + 128]
                        mm = nc.tensor.matmul(v, maxima[:, 4 + j:5 + j].broadcast_to([128, 128]), ni,
                                              start=False, stop=True, skip_group_check=True)
                mm.then_inc(shc_ok, 1)

            def slot_sums(b):
                after(pe, ed_ok, count(b, 1, 1))
                for c in range(NCH):
                    for j in range(TILES):
                        mm = nc.tensor.matmul(x01[:, c // 2, 129 * (c % 2):129 * (c % 2) + 129],
                                              disp[:, j, 128 * c:128 * c + 128], xg[:, b[1], j, :],
                                              start=(j == 0), stop=(j == TILES - 1), skip_group_check=True)
                mm.then_inc(sl_ok, 1)

            def slots_transposed(b):
                after(pe, slv_ok, count(b, 1, 1))
                for c in range(NCH):
                    mm = nc.tensor.transpose(x01[:, 0, 128 * c:128 * c + 128], slot_v[:, c, :], ident[:, :])
                mm.then_inc(slt_ok, 1)

            def hidden(b, nxt, half):
                if half == 0:
                    after(pe, sll_ok, count(b, 1, 1))
                    after(pe, slh_ok, count(b, 1, 1))
                elif nxt:
                    after(pe, stq_ok, count(b, 1, 2))
                    after(pe, stk_ok, count(b, 1, 2))
                else:
                    after(pe, ec_ok, count(b, 1, 1))
                for m in (2 * half, 2 * half + 1):
                    sl = slice(128 * m, 128 * m + 128)
                    mm = three((x01, x23)[half][:, m % 2, :], w1_hi[:, sl], w1_lo[:, sl], slot_hi[:, :],
                               slot_lo[:, :], True, True)
                mm.then_inc(hd_ok, 1)

            def processed(b):
                after(pe, ge_ok, count(b, 2, 2))
                for m in range(MCH):
                    for c in range(NCH):
                        mm = nc.tensor.matmul(x23[:, 1, 128 * c:128 * c + 128], hid_t[:, m, 128 * c:128 * c + 128],
                                              w2_sb[:, m, :], start=(m == 0 and c == 0), stop=(m == MCH - 1),
                                              skip_group_check=True)
                mm.then_inc(pr_ok, 1)

            def combine(b):
                after(pe, prs_ok, count(b, 1, 1))
                after(pe, ec_ok, count(b, 1, 1))
                for j in range(TILES):
                    for c in range(NCH):
                        mm = nc.tensor.matmul(x23[:, 0, 129 * j:129 * j + 129], comb_t[:, c, 128 * j:128 * j + 128],
                                              proc[:, c, :], start=(c == 0), stop=(c == NCH - 1),
                                              skip_group_check=True)
                mm.then_inc(fi_ok, 1)

            b0 = (0, 0)
            pe.wait_ge(pool_id, 5)
            transposes(b0)
            pe.wait_ge(wq_split, 2)
            qkv_product(b0)
            stacks(b0)
            pe.wait_ge(om_s, 3)
            project(b0, 0)
            pe.wait_ge(se_ok, 1)
            pe.wait_ge(qkvs_ok, 1)
            for c in range(NCH):
                mm = nc.tensor.transpose(x01[:, 0, 128 * c:128 * c + 128], se_n[:, c, :], ident[:, :])
            mm.then_inc(se_t, 1)
            project(b0, 1)
            pe.wait_ge(vz_const, 2)
            pe.wait_ge(se_l, 1)

            def row(b, first, nxt, nxt2):
                b1, bp = step(b, 1), step(b, -1)
                for s in range(8):
                    scores(b, s)
                    if s == 0:
                        if not first:
                            context(bp, 7)
                        if nxt:
                            transposes(b1)
                        if not first:
                            processed(bp)
                    if s == 1:
                        if nxt:
                            qkv_product(b1)
                        if not first:
                            combine(bp)
                    if s == 4:
                        slot_sums(b)
                    if s > 0:
                        context(b, s - 1)
                    if s == 1 and not first:
                        attention_out(bp)
                    if s == 2:
                        if first:
                            pe.wait_ge(w1_split, 2)
                            pe.wait_ge(d_late, 16 * LATE)
                        logits(b, nxt)
                    if s == 3:
                        shift(b)
                    if s == 5:
                        if nxt:
                            stacks(b1)
                        slots_transposed(b)
                    if s == 6:
                        hidden(b, nxt, 0)
                        if nxt:
                            project(b1, 0)
                        hidden(b, nxt, 1)
                    if s < 6:
                        project(b, s + 2)
                    elif s == 7 and nxt:
                        project(b1, 1)

            run_rows(pe, row)
            last_row = (B // 2 - 1, 1)
            processed(last_row)
            context(last_row, 7)
            combine(last_row)
            attention_out(last_row)


_INS = ['L0_attn_x', 'L0_attn_Wqkv', 'L0_attn_bqkv', 'L0_attn_Wout', 'L0_attn_bout', 'L0_attn_omega',
        'L0_attn_quad_nodes', 'L0_attn_quad_weights', 'L0_ffn_gamma_x', 'L0_ffn_gamma_slot',
        'L0_ffn_slot_embeds', 'L0_ffn_w1', 'L0_ffn_w2']


def kernel(**inputs):
    import numpy as _np
    import concourse.bacc as _bacc
    from concourse import mybir as _mybir
    from concourse.bass_utils import run_bass_kernel_spmd as _run

    nc = _bacc.Bacc("TRN2", target_bir_lowering=False, num_devices=1)
    shapes = {'L0_attn_x': (B * T, C), 'L0_ffn_slot_embeds': (SLOTS, C)}
    arrays, args = {}, []
    for name in _INS:
        a = _np.ascontiguousarray(inputs[name])
        if name in shapes:
            a = a.reshape(shapes[name])
        arrays[f"in_{name}_dram"] = a
        args.append(nc.dram_tensor(f"in_{name}_dram", a.shape, _mybir.dt.from_np(a.dtype), kind="ExternalInput").ap())
    args.append(nc.dram_tensor("out_0_dram", (B * T, C), _mybir.dt.float32, kind="ExternalOutput").ap())
    build(nc, *args)
    r = _run(nc, [arrays], core_ids=[0])
    return r.results[0]["out_0_dram"].reshape(B, T, C)
```
